# Optimizing a Trainium2 kernel written in Bass

```python
import numpy as np
import jax
import jax.numpy as jnp

def _softmax(x, axis=-1):
    return jax.nn.softmax(x, axis=axis)

def _gelu(x):
    return jax.nn.gelu(x, approximate=True)

def _silu(x):
    return jax.nn.silu(x)

def _sigmoid(x):
    return jax.nn.sigmoid(x)

def _layernorm(x, axis=-1, eps=1e-05):
    m = jnp.mean(x, axis=axis, keepdims=True)
    v = jnp.var(x, axis=axis, keepdims=True)
    return (x - m) / jnp.sqrt(v + eps)

def _scatter_add(tgt, idx, src, axis=0):
    return tgt.at[idx].add(src)

def _segment_sum(src, seg, n):
    return jax.ops.segment_sum(src, seg, n)
kernel_name = 'mk_prb_d1_jaxref_r8_ab6775'

def setup_inputs(seed: int=0):
    np.random.seed(seed)
    _w = jnp.asarray

    def _L0_attn_setup():
        import jax, jax.numpy as jnp
        import numpy as np
        NUM_HEADS = 16
        PAD_ID = 0.0
        key = jax.random.key(seed)
        ks = jax.random.split(key, 9)
        B, T, C = (2, 256, 128)
        x = jax.random.normal(ks[0], (B, T, C), dtype=jnp.float32)
        lim = (6.0 / (C + C)) ** 0.5

        def w(k):
            return jax.random.uniform(k, (C, C), dtype=jnp.float32, minval=-lim, maxval=lim)

        def b(k):
            return jax.random.uniform(k, (C,), dtype=jnp.float32)
        return {'x': x, 'wq_w': w(ks[1]), 'wq_b': b(ks[2]), 'wk_w': w(ks[3]), 'wk_b': b(ks[4]), 'wv_w': w(ks[5]), 'wv_b': b(ks[6]), 'wo_w': w(ks[7]), 'wo_b': b(ks[8])}
    _L0_attn_in = _L0_attn_setup()

    def _L0_ffn_setup():
        import jax, jax.numpy as jnp
        import numpy as np
        N_EXP = 8
        TOP_K = 2
        CAPACITY_FACTOR = 1.25
        key = jax.random.key(seed)
        ks = jax.random.split(key, 5)
        B, T, D = (4, 128, 128)
        H = 4 * D
        E = N_EXP
        x = jax.random.normal(ks[0], (B, T, D), jnp.float32)
        gate_w = jax.random.normal(ks[1], (D, E), jnp.float32) * 0.02
        c_fc = jax.random.normal(ks[2], (E, D, H), jnp.float32) * 0.02
        fc_bias = jnp.zeros((E, 1, H), jnp.float32)
        c_proj = jax.random.normal(ks[3], (E, H, D), jnp.float32) * 0.02
        proj_bias = jnp.zeros((E, 1, D), jnp.float32)
        return dict(x=x, gate_w=gate_w, c_fc=c_fc, fc_bias=fc_bias, c_proj=c_proj, proj_bias=proj_bias)
    _L0_ffn_in = _L0_ffn_setup()
    _d = {'L0_attn_x': _L0_attn_in['x'], 'L0_attn_wq_w': _L0_attn_in['wq_w'], 'L0_attn_wq_b': _L0_attn_in['wq_b'], 'L0_attn_wk_w': _L0_attn_in['wk_w'], 'L0_attn_wk_b': _L0_attn_in['wk_b'], 'L0_attn_wv_w': _L0_attn_in['wv_w'], 'L0_attn_wv_b': _L0_attn_in['wv_b'], 'L0_attn_wo_w': _L0_attn_in['wo_w'], 'L0_attn_wo_b': _L0_attn_in['wo_b'], 'L0_ffn_gate_w': _L0_ffn_in['gate_w'], 'L0_ffn_c_fc': _L0_ffn_in['c_fc'], 'L0_ffn_fc_bias': _L0_ffn_in['fc_bias'], 'L0_ffn_c_proj': _L0_ffn_in['c_proj'], 'L0_ffn_proj_bias': _L0_ffn_in['proj_bias']}
    _x0 = _d['L0_attn_x']
    _d['L0_attn_x'] = jax.random.normal(jax.random.fold_in(jax.random.key(seed), 1), (8, 512, 128), dtype=_x0.dtype)
    del _x0
    return _d

def reference(L0_attn_x, L0_attn_wq_w, L0_attn_wq_b, L0_attn_wk_w, L0_attn_wk_b, L0_attn_wv_w, L0_attn_wv_b, L0_attn_wo_w, L0_attn_wo_b, L0_ffn_gate_w, L0_ffn_c_fc, L0_ffn_fc_bias, L0_ffn_c_proj, L0_ffn_proj_bias):

    def _L0_attn_ref(x, wq_w, wq_b, wk_w, wk_b, wv_w, wv_b, wo_w, wo_b):
        import jax, jax.numpy as jnp
        import numpy as np
        NUM_HEADS = 16
        PAD_ID = 0.0
        B, T, C = x.shape
        H = NUM_HEADS
        Dh = C // H
        scale = Dh ** (-0.5)
        q = (x @ wq_w.T + wq_b).reshape(B, T, H, Dh)
        k = (x @ wk_w.T + wk_b).reshape(B, T, H, Dh)
        v = (x @ wv_w.T + wv_b).reshape(B, T, H, Dh)
        scores = jnp.einsum('bthd,bshd->bhts', q, k) * scale
        key_mask = (x[:, :, 0] != PAD_ID)[:, None, None, :]
        scores = jnp.where(key_mask, scores, -jnp.inf)
        attn = jax.nn.softmax(scores, axis=-1)
        out = jnp.einsum('bhts,bshd->bthd', attn, v).reshape(B, T, C)
        return out @ wo_w.T + wo_b

    def _L0_ffn_ref(x, gate_w, c_fc, fc_bias, c_proj, proj_bias):
        import jax, jax.numpy as jnp
        import numpy as np
        N_EXP = 8
        TOP_K = 2
        CAPACITY_FACTOR = 1.25
        B, T, D = x.shape
        n = B * T
        E, k = (N_EXP, TOP_K)
        cap = int(CAPACITY_FACTOR * n * k / E)
        xt = x.reshape(n, D)
        logits = xt @ gate_w
        top_logits, top_idx = jax.lax.top_k(logits, k)
        masked = jnp.full_like(logits, -jnp.inf)
        masked = masked.at[jnp.arange(n)[:, None], top_idx].set(top_logits)
        router_probs = jax.nn.softmax(masked, axis=-1)
        exp_mask = jax.nn.one_hot(top_idx, E, dtype=jnp.int32)
        exp_mask = jnp.transpose(exp_mask, (1, 0, 2))
        exp_rank = jnp.cumsum(exp_mask.reshape(k * n, E), axis=0) - 1
        exp_rank = exp_rank.reshape(k, n, E)
        exp_mask = exp_mask * (exp_rank < cap).astype(jnp.int32)
        used_capacity = jnp.sum(exp_mask, axis=(0, 1))
        exp_rank = jnp.sum(exp_mask * exp_rank, axis=-1)
        exp_weights = exp_mask.astype(x.dtype) * router_probs[None]
        rank_oh = jax.nn.one_hot(exp_rank, cap, dtype=x.dtype)
        cb_weight = jnp.einsum('kne,knc->nec', exp_weights, rank_oh)
        sec_mask = (cb_weight != 0).astype(x.dtype)
        exp_batches = jnp.einsum('nec,nd->ecd', sec_mask, xt)
        h = jnp.einsum('ecd,edh->ech', exp_batches, c_fc) + fc_bias
        h = jax.nn.gelu(h, approximate=False)
        exp_out = jnp.einsum('ech,ehd->ecd', h, c_proj) + proj_bias
        out = jnp.einsum('nec,ecd->nd', cb_weight, exp_out)
        return out.reshape(B, T, D)
    x = L0_attn_x
    xn = _layernorm(x, axis=-1)
    x = x + _L0_attn_ref(xn, L0_attn_wq_w, L0_attn_wq_b, L0_attn_wk_w, L0_attn_wk_b, L0_attn_wv_w, L0_attn_wv_b, L0_attn_wo_w, L0_attn_wo_b) + _L0_ffn_ref(xn, L0_ffn_gate_w, L0_ffn_c_fc, L0_ffn_fc_bias, L0_ffn_c_proj, L0_ffn_proj_bias)
    return x

_drawn_inputs = setup_inputs


def setup_inputs(seed=0):
    import zlib

    import numpy as np

    out = dict(_drawn_inputs(seed))
    spreads = {'L0_ffn_fc_bias': (0.0, 0.625), 'L0_ffn_proj_bias': (0.0, 0.1)}
    factors = {'L0_attn_wk_b': 8.0}
    for name, (base, spread) in spreads.items():
        noise = np.random.default_rng([zlib.crc32(name.encode()), seed]).standard_normal(out[name].shape)
        drawn = base * np.exp(spread * noise) if base else spread * noise
        out[name] = jnp.asarray(drawn.astype(out[name].dtype))
    for name, factor in factors.items():
        out[name] = (out[name] * factor).astype(out[name].dtype)
    return out
```

```python
from contextlib import ExitStack

import concourse.bass as bass
from concourse import mybir
from concourse.alu_op_type import AluOpType as ALU

F32 = mybir.dt.float32
F32R = mybir.dt.float32r
I32 = mybir.dt.int32
ACT = mybir.ActivationFunctionType
AX = mybir.AxisListType

P = 128
B, T, C = 8, 512, 128
H, DH = 16, 8
E, TOPK = 8, 2
HID = 4 * C
N = B * T
CAP = int(1.25 * N * TOPK / E)
SLOTS = E * CAP
NT = N // P
TT = T // P
HC = HID // P
ST = CAP // P
SCALE = float(DH) ** -0.5
EPS = 1e-5
MASKED = -float(2 ** 100)
UH = 8
UNITS = H // UH
GROUPS = 2 * TT
GB = UNITS * GROUPS
HALVES = 2 * UNITS
ROWS = 4 * DH
TAIL = 2 * ROWS
MASKROW = TAIL + 4
BIGSLOT = 4.0 * SLOTS
CH = [(0, 512), (512, 512), (1024, 256)]
NCH = len(CH)
KN = TOPK * NT
EXPERTS_FROM, EXPERTS_TO = 2, 6
assert 2 * (EXPERTS_TO - EXPERTS_FROM) == E
N_CONST = 13
WR_DMAS, LOAD_DMAS, ZERO_DMAS = 4, 5, 4
D_FIRST = (GROUPS + 4) * TT
D_TURN = GB * TT + 4
D_EXPERTS = 2 * 2 * NCH
D_EXPERTS_FROM = D_FIRST + EXPERTS_FROM * D_TURN + D_TURN


class Count:

    def __init__(self, base=0):
        self.base, self.local, self.turn, self.per = base, 0, None, 0

    def enter(self, turn, per):
        self.base, self.local = self.base + self.local, 0
        self.turn, self.per = turn, per

    def leave(self, turns):
        assert self.local == self.per, (self.local, self.per)
        self.base, self.local, self.turn = self.base + turns * self.per, 0, None

    def step(self, k=1):
        self.local += k

    def least(self, k=0):
        return self.base + self.local + k

    def value(self, k=0):
        if self.turn is None:
            return self.least(k)
        return self.turn * self.per + self.least(k)


def build(nc, x, wq, wk, wv, gate, wo, bq, bk, bv, bo, c_fc, fcb, c_proj, pjb, ident_d, prefix_d, keys_d, tail_d, out):
    with ExitStack() as ctx:
        def sb(name, shape, dt=F32):
            return ctx.enter_context(nc.sbuf_tensor(name, shape, dt))

        def ps(name):
            return ctx.enter_context(nc.psum_tensor(name, [P, 512], F32))

        def sem(name):
            return ctx.enter_context(nc.semaphore(name))

        q_stack = nc.dram_tensor("q_stack", [B, H * ROWS, T], F32, kind="Internal").ap()
        k_stack = nc.dram_tensor("k_stack", [B, H * ROWS, T], F32, kind="Internal").ap()
        mask_row = nc.dram_tensor("mask_row", [B, T], F32, kind="Internal").ap()
        slot_x = nc.dram_tensor("slot_x", [SLOTS, C], F32, kind="Internal").ap()
        slot_y = nc.dram_tensor("slot_y", [SLOTS, C], F32, kind="Internal").ap()

        ident = sb("ident", [P, P])
        prefix = sb("prefix", [P, P])
        ones = sb("ones", [P, P])
        keys = sb("keys", [P, 2 * E])
        tail = sb("tail", [P, 3])
        wq_s, wk_s, wo_s = sb("wq_s", [C, C]), sb("wk_s", [C, C]), sb("wo_s", [C, C])
        wvg_s = sb("wvg_s", [C, C + E])
        bq_s, bk_s = sb("bq_s", [C, 1]), sb("bk_s", [C, 1])
        bv_s, bo_s = sb("bv_s", [P, C]), sb("bo_s", [P, C])
        acc = sb("acc", [P, NT, C])
        xn_all = sb("xn_all", [P, NT, C])
        v_all = sb("v_all", [P, NT, C])
        K = [sb(f"K{u}", [P, UH, T], F32R) for u in range(UNITS)]
        Q = [sb(f"Q{u}", [P, UH // 2, T], F32R) for u in range(UNITS)]
        zeros4 = sb("zeros4", [4, 2, T], F32R)
        probs = sb("probs", [P, 8, T])
        v_aug = sb("v_aug", [P, TT, H, 32])
        nmax = [sb(f"nmax{q}", [P, TT, 4]) for q in range(2)]
        nmhl = [sb(f"nmhl{q}", [P, TT, 4, 2], F32R) for q in range(2)]
        nmT = [sb(f"nmT{q}", [8, T], F32R) for q in range(2)]
        pv_s = sb("pv_s", [P, T])
        rsum = sb("rsum", [P, TT, 4, 2])
        attn = sb("attn", [P, TT, C])
        attnT = sb("attnT", [C, T])
        hid = sb("hid", [P, HC, CAP])
        xe = sb("xe", [P, ST, C])
        xeT = sb("xeT", [C, CAP])
        ye = sb("ye", [P, ST, C])
        wfc = [sb(f"wfc{q}", [C, HID]) for q in range(2)]
        wpj = [sb(f"wpj{q}", [P, HC, C]) for q in range(2)]
        fcb_s = [sb(f"fcb{q}", [P, HC]) for q in range(2)]
        pjb_s = [sb(f"pjb{q}", [P, C]) for q in range(2)]
        hid_f = hid[:, :, :].rearrange("p a b -> p (a b)")
        parts = {(w, q): hid_f[:, (2 * w + q) * 2 * T:(2 * w + q + 1) * 2 * T].rearrange("p (s t) -> p s t", s=2)
                 for w in range(2) for q in range(2)}
        xst = [xe[:, TT * q:TT * (q + 1), :] for q in range(2)]
        xT = [xeT[:, T * q:T * (q + 1)] for q in range(2)]
        stats = [sb(f"stats{q}", [P, TT, 6]) for q in range(2)]
        mv = [sb(f"mv{q}", [P, TT, 2]) for q in range(2)]
        var = [sb(f"var{q}", [P, TT]) for q in range(2)]
        std = [sb(f"std{q}", [P, TT]) for q in range(2)]
        rstd = [sb(f"rstd{q}", [P, TT]) for q in range(2)]
        mrow = [sb(f"mrow{q}", [1, T], F32R) for q in range(2)]
        logit = sb("logit", [P, NT, E])
        r_eq = sb("r_eq", [P, NT, E])
        r_key = sb("r_key", [P, NT, E])
        top = sb("top", [P, TOPK, NT])
        kmax = sb("kmax", [P, NT])
        hot = sb("hot", [P, KN, E])
        scan = sb("scan", [P, KN, E])
        rank = sb("rank", [P, KN, E])
        r_at = sb("r_at", [P, KN])
        r_base = sb("r_base", [P, KN])
        keep = sb("keep", [P, KN])
        gap = sb("gap", [P, NT])
        prob = sb("prob", [P, KN])
        wgt = sb("wgt", [P, KN])
        slot_f = sb("slot_f", [P, KN])
        put_f = sb("put_f", [P, KN])
        put_i = sb("put_i", [P, KN], I32)
        get_i = sb("get_i", [P, KN], I32)

        bA = [ps(f"bA{n}") for n in range(4)]
        bD = [ps(f"bD{n}") for n in range(2)]
        bPV = ps("bPV")
        bX = ps("bX")

        s_const = sem("s_const")
        s_fill = sem("s_fill")
        s_rows = sem("s_rows")
        s_xin = [sem("s_xin0"), sem("s_xin1")]
        s_var = sem("s_var")
        s_std = sem("s_std")
        s_xn = sem("s_xn")
        s_copy = sem("s_copy")
        s_tp = sem("s_tp")
        s_xT = sem("s_xT")
        s_qk = sem("s_qk")
        s_hi = sem("s_hi")
        s_lo = sem("s_lo")
        s_vg = sem("s_vg")
        s_ve = sem("s_ve")
        s_mask = sem("s_mask")
        s_wr = [sem("s_wr0"), sem("s_wr1")]
        s_hot = sem("s_hot")
        s_rank = sem("s_rank")
        s_gap = sem("s_gap")
        s_gexp = sem("s_gexp")
        s_route = sem("s_route")
        s_put = sem("s_put")
        s_chain = sem("s_chain")
        s_load = [[sem(f"s_load{u}{q}") for q in range(2)] for u in range(UNITS)]
        s_st = sem("s_st")
        s_exp = sem("s_exp")
        s_pv = sem("s_pv")
        s_pvo = sem("s_pvo")
        s_d = sem("s_d")
        s_dd = sem("s_dd")
        s_nm = sem("s_nm")
        s_nt = sem("s_nt")
        s_ne = sem("s_ne")
        s_nq = [sem("s_nq0"), sem("s_nq1")]
        s_vaug = sem("s_vaug")
        s_w = [sem("s_w0"), sem("s_w1")]
        s_xe = sem("s_xe")
        s_up = sem("s_up")
        s_ge = sem("s_ge")
        s_zero = sem("s_zero")
        s_slot = sem("s_slot")
        s_get = [sem(f"s_get{n}") for n in range(4)]
        s_comb = sem("s_comb")
        s_out = sem("s_out")

        x_v = x.rearrange("(n p) c -> p n c", p=P)
        out_v = out.rearrange("(n p) c -> p n c", p=P)
        slot_x_v = slot_x.rearrange("(e s p) c -> e p s c", s=ST, p=P)
        slot_y_v = slot_y.rearrange("(e s p) c -> e p s c", s=ST, p=P)

        def rows(t, b, k=0, n=TT):
            return t[:, bass.ds(b * TT + k, n), :]

        def wait(eng, s, value):
            if not isinstance(value, int) or value > 0:
                eng.wait_ge(s, value)

        def each_batch(eng, step):
            for q in range(2):
                step(q, q)
            with eng.Fori(1, B // 2) as i:
                for q in range(2):
                    step(i * 2 + q, q)

        def each_turn(eng, counts, turn):
            for start, end, experts in ((0, EXPERTS_FROM, False), (EXPERTS_FROM, EXPERTS_TO, True)):
                with eng.Fori(start, end) as b:
                    for c, per, more in counts:
                        c.enter(b - start if start else b, per + more * experts)
                    turn(b, experts, False)
                for c, _, _ in counts:
                    c.leave(end - start)
            for b in range(EXPERTS_TO, B):
                turn(b, False, b == B - 1)

        block = ctx.enter_context(nc.Block())

        @block.sync
        def _(sp):
            for t, src in ((ident, ident_d), (wq_s, wq), (wk_s, wk), (bq_s, bq), (bk_s, bk), (tail, tail_d),
                           (prefix, prefix_d), (keys, keys_d), (wo_s, wo)):
                sp.dma_start(t[:], src).then_inc(s_const, 16)
            sp.dma_start(wvg_s[:, 0:C], wv).then_inc(s_const, 16)
            sp.dma_start(wvg_s[:, C:C + E], gate).then_inc(s_const, 16)
            sp.dma_start(bv_s[:], bv.to_broadcast([P, C])).then_inc(s_const, 16)
            sp.dma_start(bo_s[:], bo.to_broadcast([P, C])).then_inc(s_const, 16)

            def load_x(b, q):
                sp.dma_start(rows(acc, b), rows(x_v, b)).then_inc(s_xin[q], 16)

            def write_stacks(b, q):
                sp.wait_ge(s_lo, b * 2 + 2)
                pq = parts[0, q].rearrange("p s t -> p (s t)")
                pk = parts[1, q]
                dq = q_stack[b].rearrange("(c r s) t -> c r (s t)", r=2, s=2)
                dk = k_stack[b].rearrange("(c s) t -> c s t", s=4)
                sp.dma_start(dq, pq[:, None, :].to_broadcast([P, 2, 2 * T])).then_inc(s_wr[q], 16)
                for s in range(2):
                    sp.dma_start(dk[:, 2 * s:2 * s + 2, :], pk[:, s:s + 1, :].to_broadcast([P, 2, T])).then_inc(s_wr[q], 16)
                sp.wait_ge(s_mask, b + 1)
                sp.dma_start(mask_row[bass.ds(b, 1), :], mrow[q][:].bitcast(F32)).then_inc(s_wr[q], 16)

            load_x(0, 0)
            load_x(1, 1)

            with sp.Fori(0, B // 2 - 1) as i:
                for q in range(2):
                    sp.wait_ge(s_xn, i * 2 + q + 1)
                    load_x(i * 2 + q + 2, q)
                    write_stacks(i * 2 + q, q)
            for q in range(2):
                write_stacks(B - 2 + q, q)

            def load_quad(b, u, q):
                pair0 = u * (UH // 2) + 2 * q
                qs = q_stack[b].rearrange("(pair r) t -> r pair t", r=2 * ROWS)
                ks = k_stack[b].rearrange("(pair e r) t -> e r pair t", e=2, r=ROWS)
                kd = K[u][:, 4 * q:4 * q + 4, :].bitcast(F32).rearrange("p (pair e) t -> p e pair t", e=2)
                sp.dma_start(Q[u][0:2 * ROWS, 2 * q:2 * q + 2, :].bitcast(F32), qs[:, pair0:pair0 + 2, :]).then_inc(s_load[u][q], 16)
                for e in range(2):
                    sp.dma_start(kd[e * ROWS:(e + 1) * ROWS, e, :, :], ks[e, :, pair0:pair0 + 2, :]
                                 ).then_inc(s_load[u][q], 16)
                sp.dma_start(K[u][MASKROW:MASKROW + 1, 4 * q:4 * q + 4, :].bitcast(F32),
                             mask_row[bass.ds(b, 1), None, :].to_broadcast([1, 4, T])).then_inc(s_load[u][q], 16)
                sp.dma_start(Q[u][TAIL:TAIL + 4, 2 * q:2 * q + 2, :].bitcast(F32), zeros4[:].bitcast(F32)).then_inc(s_load[u][q], 16)

            def max_rows(u, q, m):
                sp.wait_ge(s_ne, m + 1)
                for pair in range(2):
                    sp.dma_start(Q[u][TAIL:TAIL + 4, 2 * q + pair, :].bitcast(F32),
                                 nmT[q][4 * pair:4 * pair + 4, :].bitcast(F32)).then_inc(s_nq[q], 16)

            sp.wait_ge(s_rows, 1)
            for q in range(2):
                sp.wait_ge(s_wr[q], B // 2 * WR_DMAS * 16)
            for u in range(UNITS):
                for q in range(2):
                    load_quad(0, u, q)
            for q in range(2):
                max_rows(0, q, q)

            def load_rows(e):
                sp.dma_start(xe[:], slot_x_v[e]).then_inc(s_xe, 16)

            def load_experts(b):
                e = b * 2 - 2 * EXPERTS_FROM
                sp.wait_ge(s_put, KN * 16)
                load_rows(e)
                for q in range(2):
                    sp.dma_start(wfc[q][:], c_fc[e + q]).then_inc(s_w[q], 16)
                    sp.dma_start(wpj[q][:], c_pj_v[e + q]).then_inc(s_w[q], 16)
                    sp.dma_start(fcb_s[q][:], fcb[e + q]).then_inc(s_w[q], 16)
                    sp.dma_start(pjb_s[q][:], pjb[e + q].to_broadcast([P, C])).then_inc(s_w[q], 16)

            def experts(b):
                for q in range(2):
                    e = b * 2 - 2 * EXPERTS_FROM + q
                    before = (b - EXPERTS_FROM) * (D_TURN + D_EXPERTS) + D_EXPERTS_FROM + q * 2 * NCH
                    if q == 0:
                        sp.wait_ge(s_dd, before + NCH)
                        load_rows(e + 1)
                    sp.wait_ge(s_dd, before + 2 * NCH)
                    sp.dma_start(slot_y_v[e], ye[:]).then_inc(s_slot, 16)

            c_pj_v = c_proj.rearrange("e (h p) c -> e p h c", p=P)

            def turn(b, with_experts, last):
                if with_experts:
                    load_experts(b)
                through = b * (4 * GB)
                m = b * HALVES + 2
                max_rows(1, 0, m)
                if last:
                    max_rows(1, 1, m + 1)
                    return
                sp.wait_ge(s_st, through + 4 * 4)
                load_quad(b + 1, 0, 0)
                sp.wait_ge(s_st, through + 4 * 8)
                load_quad(b + 1, 0, 1)
                max_rows(1, 1, m + 1)
                sp.wait_ge(s_st, through + 4 * 12)
                load_quad(b + 1, 1, 0)
                max_rows(0, 0, m + 2)
                sp.wait_ge(s_st, through + 4 * 16)
                load_quad(b + 1, 1, 1)
                max_rows(0, 1, m + 3)
                if with_experts:
                    experts(b)

            each_turn(sp, [], turn)
            for b in range(B):
                sp.wait_ge(s_comb, b + 1)
                sp.dma_start(rows(out_v, b), rows(acc, b)).then_inc(s_out, 16)
            sp.wait_ge(s_out, B * 16)

        @block.gpsimd
        def _(pool):
            nc.gpsimd.memset(probs[:], 0.0).then_inc(s_fill, 1)
            pool.wait_ge(s_fill, 1)
            per = SLOTS * C // P // ZERO_DMAS
            pz = probs[:].rearrange("p a b -> p (a b)")
            for h in range(ZERO_DMAS):
                pool.dma_start(slot_x.rearrange("(p h r) c -> h p (r c)", p=P, h=ZERO_DMAS)[h], pz[:, 0:per]
                               ).then_inc(s_zero, 16)
            for t in (K[0], Q[0], K[1], Q[1]):
                nc.gpsimd.memset(t[:].bitcast(F32), 0.0).then_inc(s_fill, 1)
            nc.gpsimd.memset(v_aug[:], 0.0).then_inc(s_fill, 1)
            nc.gpsimd.memset(zeros4[:].bitcast(F32), 0.0).then_inc(s_fill, 1)
            pool.wait_ge(s_const, N_CONST * 16)

            def front(b, q):
                pool.wait_ge(s_xn, b + 1)
                nc.gpsimd.tensor_copy(rows(xn_all, b), xst[q])
                nc.gpsimd.tensor_tensor(rows(acc, b), rows(acc, b), bo_s[:, None, :].to_broadcast([P, TT, C]),
                                        ALU.add).then_inc(s_copy, 1)

            each_batch(pool, front)

            pool.wait_ge(s_route, 1)
            pool.wait_ge(s_copy, B)
            pool.wait_ge(s_zero, ZERO_DMAS * 16)
            for k in range(TOPK):
                for n in range(NT):
                    col = k * NT + n
                    pool.indirect_dma_start(slot_x, bass.IndirectOffsetOnAxis(ap=put_i[:, col:col + 1], axis=0),
                                            xn_all[:, n, :], None, bounds_check=SLOTS - 1, oob_is_err=False
                                            ).then_inc(s_put, 16)
            pool.wait_ge(s_slot, E * 16 + 16)
            for b in range(B):
                if b >= 4:
                    pool.wait_ge(s_comb, b - 3)
                for k in range(TOPK):
                    for n in range(TT):
                        col = k * NT + b * TT + n
                        pool.indirect_dma_start(xn_all[:, (b % 4) * 2 * TT + k * TT + n, :], None, slot_y,
                                                bass.IndirectOffsetOnAxis(ap=get_i[:, col:col + 1], axis=0),
                                                bounds_check=SLOTS - 1, oob_is_err=False).then_inc(s_get[b % 4], 16)
            for n in range(4):
                pool.wait_ge(s_get[n], (B // 4) * TOPK * TT * 16)

        @block.scalar
        def _(act):
            def high(b, q):
                wait(act, s_wr[q], (b - q) * (WR_DMAS * 16 // 2))
                for w, bias in ((0, bq_s), (1, bk_s)):
                    act.wait_ge(s_qk, b * 2 + w + 1)
                    nc.scalar.activation(parts[w, q][:, 0, :].bitcast(F32R), bA[2 + w][:], ACT.Identity, bias=bias[:]
                                         ).then_inc(s_hi, 1)

            def front(b, q):
                act.wait_ge(s_var, b + 1)
                nc.scalar.activation(std[q][:], var[q][:], ACT.Sqrt).then_inc(s_std, 1)
                act.wait_ge(s_tp, b + 1)
                wait(act, s_vg, (b - 1) * 2)
                wait(act, s_mask, b - 1)
                nc.scalar.copy(xT[q], bA[q][:]).then_inc(s_xT, 1)
                if not isinstance(b, int) or b > 0:
                    high(b - 1, 1 - q)

            act.wait_ge(s_const, N_CONST * 16)
            each_batch(act, front)
            high(B - 1, 1)
            act.wait_ge(s_gap, 1)
            nc.scalar.activation(gap[:], gap[:], ACT.Exp).then_inc(s_gexp, 1)
            act.wait_ge(s_zero, ZERO_DMAS * 16)

            def maxima(m, q, k):
                act.wait_ge(s_nt, m + 1)
                wait(act, s_nq[q], k * 32)
                nc.scalar.copy(nmT[q][:], bX[0:8, :]).then_inc(s_ne, 1)

            def group(b, g):
                n = b * GB + g
                for h in range(4):
                    act.wait_ge(s_st, n * 4 + h + 1)
                    if h == 0:
                        wait(act, s_pv, n - 1)
                    nc.scalar.activation(probs[:, (g % 2) * 4 + h, :], bA[h][:], ACT.Exp, scale=SCALE).then_inc(s_exp, 1)
                if g % 4 == 0:
                    m = b * HALVES + g // 4 + 1
                    maxima(m, (g // 4 + 1) % 2, b * 2 + (g // 4 + 1) // 2)

            def sums(unit):
                act.wait_ge(s_pv, (unit + 1) * GROUPS)
                nc.scalar.copy(pv_s[:], bPV[:]).then_inc(s_pvo, 1)

            def experts(b):
                for q in range(2):
                    e = b * 2 - 2 * EXPERTS_FROM + q
                    for hc in range(HC):
                        for c, (c0, w) in enumerate(CH):
                            k = hc * NCH + c
                            act.wait_ge(s_up, e * (HC * NCH) + k + 1)
                            nc.scalar.activation(hid[:, hc, c0:c0 + w], bA[k % 4][:, 0:w], ACT.Gelu,
                                                 bias=fcb_s[q][:, hc:hc + 1]).then_inc(s_ge, 1)

            maxima(0, 0, 0)
            for g in range(4):
                group(0, g)

            def turn(b, with_experts, last):
                for g in range(4, GB):
                    if last and g == 12:
                        for h in range(4):
                            act.wait_ge(s_st, (b * GB + g) * 4 + h + 1)
                            if h == 0:
                                act.wait_ge(s_pv, b * GB + g - 1)
                            nc.scalar.activation(probs[:, (g % 2) * 4 + h, :], bA[h][:], ACT.Exp, scale=SCALE
                                                 ).then_inc(s_exp, 1)
                    else:
                        group(b, g)
                    if g == GROUPS:
                        sums(b * UNITS)
                if last:
                    sums(b * UNITS + 1)
                    return
                for g in range(4):
                    group(b + 1, g)
                    if g == 0:
                        sums(b * UNITS + 1)
                if with_experts:
                    experts(b)

            each_turn(act, [], turn)

        @block.vector
        def _(dve):
            chain = [0]

            def link(ins):
                ins.then_inc(s_chain, 1)
                chain[0] += 1
                dve.wait_ge(s_chain, chain[0])

            F = 3

            def norm(b, q):
                dve.wait_ge(s_xin[q], (b - q) * 8 + 16)
                for k in range(TT):
                    last = nc.vector.bn_stats(stats[q][:, k, :], rows(acc, b, k, 1).rearrange("p n c -> p (n c)"))
                last.then_inc(s_chain, 1)
                dve.wait_ge(s_chain, b * F + 1)
                nc.vector.memset(var[q][:], 0.0)
                for k in range(TT):
                    last = nc.vector.bn_aggr(mv[q][:, k, :], stats[q][:, k, :])
                last.then_inc(s_chain, 1)
                dve.wait_ge(s_chain, b * F + 2)
                nc.vector.tensor_scalar(var[q][:], mv[q][:, :, 1], EPS, None, ALU.add).then_inc(s_var, 1)
                dve.wait_ge(s_std, b + 1)
                nc.vector.reciprocal(rstd[q][:], std[q][:]).then_inc(s_chain, 1)
                dve.wait_ge(s_chain, b * F + 3)
                wait(dve, s_tp, b - 1)
                wait(dve, s_copy, b - 1)
                for k in range(TT):
                    last = nc.vector.tensor_scalar(xst[q][:, k, :], rows(acc, b, k, 1).rearrange("p n c -> p (n c)"),
                                                   mv[q][:, k, 0:1], rstd[q][:, k:k + 1], ALU.subtract, ALU.mult)
                last.then_inc(s_xn, 1)

            def late(b, q):
                for w, bias in ((0, bq_s), (1, bk_s)):
                    dve.wait_ge(s_hi, b * 2 + w + 1)
                    nc.vector.scalar_tensor_tensor(out=parts[w, q][:, 1, :].bitcast(F32R), in0=bA[2 + w][:], scalar=bias[:],
                                                   in1=parts[w, q][:, 0, :], op0=ALU.add, op1=ALU.subtract).then_inc(s_lo, 1)
                nc.vector.tensor_scalar(mrow[q][:], xT[q][0:1, :], 0.0, MASKED, ALU.is_equal, ALU.mult).then_inc(s_mask, 1)
                for h in range(2):
                    dve.wait_ge(s_vg, b * 2 + h + 1)
                    pv = bD[h][:, 0:2 * (C + E)].rearrange("p (n c) -> p n c", n=2)
                    nc.vector.tensor_tensor(rows(v_all, b, 2 * h, 2), pv[:, :, 0:C], bv_s[:, None, :].to_broadcast([P, 2, C]),
                                            ALU.add)
                    nc.vector.tensor_copy(rows(logit, b, 2 * h, 2), pv[:, :, C:C + E]).then_inc(s_ve, 1)

            def front(b, q):
                norm(b, q)
                if not isinstance(b, int) or b > 0:
                    late(b - 1, 1 - q)

            nc.vector.memset(ones[:], 1.0).then_inc(s_slot, 16)
            dve.wait_ge(s_const, N_CONST * 16)
            each_batch(dve, front)
            late(B - 1, 1)
            chain[0] = B * F

            dve.wait_ge(s_fill, 7)
            for u in range(UNITS):
                kt = K[u][TAIL:P, :, :].rearrange("p (pair e) t -> p e pair t", e=2)
                for e in range(2):
                    nc.vector.tensor_scalar(kt[:, e], kt[:, e].bitcast(F32), tail[TAIL:P, e:e + 1], None, ALU.add)
                nc.vector.tensor_scalar(Q[u][TAIL:P, :, :], Q[u][TAIL:P, :, :].bitcast(F32), tail[TAIL:P, 2:3], None, ALU.add)
            for q in range(2):
                va = v_aug[:].rearrange("p j (u r) c -> p (j u) r c", u=UNITS)
                last = nc.vector.memset(va[:, :, 4 * q:4 * q + 4, 16 + q], 1.0)
            last.then_inc(s_rows, 1)

            lg = logit[:]
            hot_k = hot[:].rearrange("p (k n) e -> p k n e", k=TOPK)
            wide = [P, NT, E]
            dve.wait_ge(s_ve, 2 * B)
            for k in range(TOPK):
                link(nc.vector.tensor_reduce(top[:, k, :], lg, AX.X, ALU.max))
                link(nc.vector.tensor_tensor(r_eq[:], lg, top[:, k, :, None].to_broadcast(wide), ALU.is_equal))
                link(nc.vector.tensor_tensor(r_key[:], r_eq[:], keys[:, None, 0:E].to_broadcast(wide), ALU.mult))
                link(nc.vector.tensor_reduce(kmax[:], r_key[:], AX.X, ALU.max))
                ins = nc.vector.tensor_tensor(hot_k[:, k], r_key[:], kmax[:, :, None].to_broadcast(wide), ALU.is_equal)
                if k == TOPK - 1:
                    ins.then_inc(s_hot, 1)
                else:
                    link(ins)
                    link(nc.vector.scalar_tensor_tensor(out=lg, in0=hot_k[:, k], scalar=MASKED, in1=lg, op0=ALU.mult,
                                                        op1=ALU.add))
            nc.vector.tensor_tensor(gap[:], top[:, 1, :], top[:, 0, :], ALU.subtract).then_inc(s_gap, 1)
            dve.wait_ge(s_rank, 1)
            total = bPV[:].rearrange("p (n e) -> p n e", e=E)
            for e in range(E):
                ins = nc.vector.tensor_tensor_scan(scan[:, :, e], ones[:, 0:KN], total[:, :, e], 0.0, ALU.mult, ALU.add)
            link(ins)
            link(nc.vector.tensor_tensor(scan[:], scan[:], total, ALU.subtract))
            link(nc.vector.tensor_tensor(rank[:], scan[:], bX[:].rearrange("p (n e) -> p n e", e=E), ALU.add))
            dve.wait_ge(s_hot, 1)
            link(nc.vector.tensor_tensor(rank[:], rank[:], hot[:], ALU.mult))
            nc.vector.tensor_reduce(r_at[:], rank[:], AX.X, ALU.add)
            link(nc.vector.tensor_tensor(scan[:], hot[:], keys[:, None, E:2 * E].to_broadcast([P, KN, E]), ALU.mult))
            nc.vector.tensor_reduce(r_base[:], scan[:], AX.X, ALU.add)
            link(nc.vector.tensor_scalar(keep[:], r_at[:], float(CAP), None, ALU.is_lt))
            link(nc.vector.tensor_tensor(slot_f[:], r_at[:], keep[:], ALU.mult))
            link(nc.vector.tensor_tensor(slot_f[:], slot_f[:], r_base[:], ALU.add))
            nc.vector.tensor_copy(get_i[:], slot_f[:])
            link(nc.vector.tensor_scalar(put_f[:], keep[:], -BIGSLOT, BIGSLOT, ALU.mult, ALU.add))
            link(nc.vector.tensor_tensor(put_f[:], put_f[:], slot_f[:], ALU.add))
            nc.vector.tensor_copy(put_i[:], put_f[:]).then_inc(s_route, 1)
            dve.wait_ge(s_gexp, 1)
            link(nc.vector.tensor_scalar(kmax[:], gap[:], 1.0, None, ALU.add))
            link(nc.vector.reciprocal(prob[:, 0:NT], kmax[:]))
            link(nc.vector.tensor_tensor(prob[:, NT:KN], prob[:, 0:NT], gap[:], ALU.mult))
            link(nc.vector.tensor_tensor(wgt[:], prob[:], keep[:], ALU.mult))

            d = Count()
            own = Count()
            own.step(chain[0])

            def chained(ins):
                ins.then_inc(s_chain, 1)
                own.step()
                dve.wait_ge(s_chain, own.value())

            def bank():
                return bD[d.least() % 2]

            def take():
                dve.wait_ge(s_d, d.value(1))

            def scores_max(s):
                q, head = (s // 4) % 2, s % 4
                for k in range(TT):
                    take()
                    nc.vector.tensor_reduce(nmax[q][:, k, head:head + 1], bank()[:], AX.X, ALU.max, negate=True
                                            ).then_inc(s_dd, 1)
                    d.step()
                if head == 3:
                    dve.wait_ge(s_dd, d.value())
                    chained(nc.vector.tensor_copy(nmhl[q][:, :, :, 0], nmax[q][:]))
                    nc.vector.tensor_tensor(nmhl[q][:, :, :, 1], nmax[q][:], nmhl[q][:, :, :, 0].bitcast(F32), ALU.subtract
                                            ).then_inc(s_nm, 1)

            def fill_v(b):
                wait(dve, s_pv, b * GB)
                va = v_aug[:].rearrange("p j (u r) c -> p (j u) r c", u=UNITS)
                vs = rows(v_all, b).rearrange("p j (u r c) -> p (j u) r c", u=UNITS, c=DH)
                for q in range(2):
                    last = nc.vector.tensor_copy(va[:, :, 4 * q:4 * q + 4, DH * q:DH * (q + 1)], vs[:, :, 4 * q:4 * q + 4, :])
                last.then_inc(s_vaug, 1)

            def normalise(u):
                take()
                src = bank()[:].rearrange("p (k c) -> p k c", c=P)
                sums = bank()[:].rearrange("p (kg c) -> p kg c", c=32)[:, :, 2 * DH:2 * DH + 2]
                chained(nc.vector.reciprocal(rsum[:].rearrange("p k g q -> p (k g) q"), sums))
                for q in range(2):
                    o = attn[:, :, u * 64 + q * 32:u * 64 + (q + 1) * 32].rearrange("p k (g c) -> p k g c", c=DH)
                    i0 = src.rearrange("p k (g c) -> p k g c", c=32)[:, :, :, DH * q:DH * (q + 1)]
                    last = nc.vector.tensor_tensor(o, i0, rsum[:, :, :, q:q + 1].to_broadcast([P, TT, 4, DH]), ALU.mult)
                last.then_inc(s_dd, 1)
                d.step()

            def take_attnT():
                take()
                nc.vector.tensor_copy(attnT[:], bank()[:]).then_inc(s_dd, 1)
                d.step()

            def take_out(b):
                take()
                nc.vector.tensor_tensor(rows(acc, b), bank()[:].rearrange("p (k c) -> p k c", c=C), rows(acc, b), ALU.add
                                        ).then_inc(s_dd, 1)
                d.step()

            def experts(b):
                for q in range(2):
                    e = b * 2 - 2 * EXPERTS_FROM + q
                    for (c0, w) in CH:
                        take()
                        nc.vector.tensor_copy(xeT[:, c0:c0 + w], bank()[:, 0:w]).then_inc(s_dd, 1)
                        d.step()
                    dve.wait_ge(s_slot, e * 16 + 16)
                    for (c0, w) in CH:
                        take()
                        k0, nk = c0 // P, w // P
                        nc.vector.tensor_tensor(ye[:, k0:k0 + nk, :], bank()[:, 0:w].rearrange("p (k c) -> p k c", c=C),
                                                pjb_s[q][:, None, :].to_broadcast([P, nk, C]), ALU.add).then_inc(s_dd, 1)
                        d.step()

            def combine(b):
                dve.wait_ge(s_get[b % 4], (b // 4 + 1) * TOPK * TT * 16)
                for k in range(TOPK):
                    for n in range(TT):
                        t, col = b * TT + n, k * NT + b * TT + n
                        last = nc.vector.scalar_tensor_tensor(out=acc[:, t, :], in0=xn_all[:, (b % 4) * 2 * TT + k * TT + n, :],
                                                              scalar=wgt[:, col:col + 1], in1=acc[:, t, :], op0=ALU.mult,
                                                              op1=ALU.add)
                    if k == 0:
                        chained(last)
                last.then_inc(s_comb, 1)


            def group(b, g, last=False, first=False):
                if g == 2:
                    fill_v(b)
                if not last or g < GROUPS:
                    scores_max(g % GROUPS)
                if g == 1 and not first:
                    normalise(1)
                if g == 2 and not first:
                    take_attnT()
                if g == 3 and not first:
                    take_out(b - 1)
                if g == GROUPS + 1:
                    normalise(0)

            for s in range(GROUPS):
                scores_max(s)
            for g in range(4):
                group(0, g, first=True)

            def turn(b, with_experts, last):
                for g in range(4, GB):
                    group(b, g, last)
                    if last and g >= GB - (B - 2):
                        combine(g - (GB - (B - 2)))
                if last:
                    normalise(1)
                    take_attnT()
                    take_out(b)
                    return
                for g in range(4):
                    group(b + 1, g)
                if with_experts:
                    experts(b)

            each_turn(dve, [(d, D_TURN, D_EXPERTS), (own, HALVES + UNITS, 0)], turn)
            dve.wait_ge(s_dd, d.value())
            for b in range(B - 2, B):
                combine(b)

        @block.tensor
        def _(pe):
            def products(b, q):
                pe.wait_ge(s_xT, b + 1)
                for w, weights in ((0, wq_s), (1, wk_s)):
                    wait(pe, s_lo, b * 2 - 1 + w)
                    nc.tensor.matmul(bA[2 + w][:], weights[:], xT[q], start=True, stop=True).then_inc(s_qk, 1)
                for h in range(2):
                    wait(pe, s_ve, b * 2 - 1 + h)
                    for n in range(2):
                        k = 2 * h + n
                        last = nc.tensor.matmul(bD[h][:, n * (C + E):(n + 1) * (C + E)], xT[q][:, k * P:(k + 1) * P], wvg_s[:],
                                                start=True, stop=True)
                    last.then_inc(s_vg, 1)

            def front(b, q):
                pe.wait_ge(s_xn, b + 1)
                wait(pe, s_xT, b - 1)
                for k in range(TT):
                    last = nc.tensor.transpose(bA[q][:, k * P:(k + 1) * P], xst[q][:, k, :], ident[:])
                last.then_inc(s_tp, 1)
                if not isinstance(b, int) or b > 0:
                    products(b - 1, 1 - q)

            pe.wait_ge(s_const, N_CONST * 16)
            each_batch(pe, front)
            products(B - 1, 1)

            pe.wait_ge(s_hot, 1)
            hot_f = hot[:].rearrange("p n e -> p (n e)")
            nc.tensor.matmul(bX[:], prefix[:], hot_f, start=True, stop=True)
            nc.tensor.matmul(bPV[:], ones[:], hot_f, start=True, stop=True).then_inc(s_rank, 1)

            d = Count()

            def free():
                if d.turn is not None or d.least() >= 2:
                    pe.wait_ge(s_dd, d.value(-1))
                return bD[d.least() % 2]

            def done(ins):
                ins.then_inc(s_d, 1)
                d.step()

            def scores_for_max(b, u, s, first, n):
                q = s // 4
                if s % 4 == 0 and first == 0:
                    pe.wait_ge(s_load[u][q], b * (LOAD_DMAS * 16) + LOAD_DMAS * 16)
                for k in range(first, first + n):
                    done(nc.tensor.matmul(free()[:], Q[u][:, s // 2, k * P:(k + 1) * P], K[u][:, s, :], start=True, stop=True))

            def maxima(m, q):
                pe.wait_ge(s_nm, m + 1)
                wait(pe, s_ne, m)
                for k in range(TT):
                    last = nc.tensor.transpose(bX[0:8, k * P:(k + 1) * P],
                                               nmhl[q][:, k, :, :].rearrange("p h s -> p (h s)").bitcast(F32), ident[:])
                last.then_inc(s_nt, 1)

            def scores(b, g, first, n):
                u, q, j = g // GROUPS, (g % GROUPS) // 4, g % 4
                if j == 0 and first == 0:
                    pe.wait_ge(s_nq[q], (b * UNITS + u) * 32 + 32)
                for h in range(first, first + n):
                    wait(pe, s_exp, (b * GB + g) * 4 - 3 + h)
                    nc.tensor.matmul(bA[h][:], K[u][:, 4 * q + h, j * P:(j + 1) * P], Q[u][:, 2 * q + h // 2, :],
                                     start=True, stop=True).then_inc(s_st, 1)

            def with_v(b, g):
                n = b * GB + g
                u, q, j = g // GROUPS, (g % GROUPS) // 4, g % 4
                pe.wait_ge(s_exp, n * 4 + 4)
                if g == 0:
                    pe.wait_ge(s_vaug, b + 1)
                if g % GROUPS == 0:
                    wait(pe, s_pvo, b * UNITS + u)
                for h in range(4):
                    last = nc.tensor.matmul(bPV[32 * h:32 * h + 32, :], v_aug[:, j, u * UH + 4 * q + h, :],
                                            probs[:, (g % 2) * 4 + h, :], start=(g % GROUPS == 0),
                                            stop=(g % GROUPS == GROUPS - 1))
                last.then_inc(s_pv, 1)

            def turned(src, n=TT):
                to = free()
                for k in range(n):
                    last = nc.tensor.transpose(to[:, k * P:(k + 1) * P], src(k), ident[:])
                done(last)

            def output_sums(b, u):
                pe.wait_ge(s_pvo, b * UNITS + u + 1)
                turned(lambda k: pv_s[:, k * P:(k + 1) * P])

            def project(since=TT):
                pe.wait_ge(s_dd, d.value(-since))
                to = free()
                for k in range(TT):
                    last = nc.tensor.matmul(to[:, k * P:(k + 1) * P], attnT[:, k * P:(k + 1) * P], wo_s[:], start=True,
                                            stop=True)
                done(last)

            def attn_turned():
                pe.wait_ge(s_dd, d.value(-TT))
                turned(lambda k: attn[:, k, :])

            def group(b, g, last=False, first=False):
                def ahead(k, n):
                    if g < GROUPS:
                        scores_for_max(b, 1, g, k, n)
                    elif not last:
                        scores_for_max(b + 1, 0, g - GROUPS, k, n)

                ahead(0, 2)
                if g >= 2:
                    with_v(b, g - 2)
                elif not first:
                    with_v(b - 1, GB - 2 + g)
                ahead(2, 1)
                scores(b, g, 0, 2)
                ahead(3, 1)
                scores(b, g, 2, 2)
                if g % 4 == 0 and not (last and g == 3 * 4):
                    maxima(b * HALVES + g // 4 + 1, (g // 4 + 1) % 2)
                if g == 1 and not first:
                    output_sums(b - 1, 1)
                if g == 2 and not first:
                    attn_turned()
                if g == 3 and not first:
                    project()
                if g == GROUPS + 1:
                    output_sums(b, 0)

            def experts(b):
                pe.wait_ge(s_exp, b * (4 * GB) + 4 * (GB + 4))
                for q in range(2):
                    e = b * 2 - 2 * EXPERTS_FROM + q
                    pe.wait_ge(s_xe, e * 16 + 16)
                    chunks = []
                    for (c0, w) in CH:
                        turned(lambda k: xe[:, c0 // P + k, :], w // P)
                        chunks.append(d.value())
                    pe.wait_ge(s_w[q], b * 64 - (EXPERTS_FROM - 1) * 64)
                    for hc in range(HC):
                        for c, (c0, w) in enumerate(CH):
                            k = hc * NCH + c
                            if hc == 0:
                                pe.wait_ge(s_dd, chunks[c])
                            if k >= 4:
                                pe.wait_ge(s_ge, e * (HC * NCH) + k - 3)
                            nc.tensor.matmul(bA[k % 4][:, 0:w], wfc[q][:, hc * P:(hc + 1) * P], xeT[:, c0:c0 + w], start=True,
                                             stop=True).then_inc(s_up, 1)
                    pe.wait_ge(s_ge, e * (HC * NCH) + HC * NCH)
                    for (c0, w) in CH:
                        to = free()
                        for k in range(w // P):
                            for hc in range(HC):
                                last = nc.tensor.matmul(to[:, k * P:(k + 1) * P], hid[:, hc, c0 + k * P:c0 + (k + 1) * P],
                                                        wpj[q][:, hc, :], start=(hc == 0), stop=(hc == HC - 1))
                        done(last)

            pe.wait_ge(s_ve, 2 * B)
            pe.wait_ge(s_rows, 1)
            for s in range(GROUPS):
                scores_for_max(0, 0, s, 0, TT)
                if s == 4:
                    pe.wait_ge(s_route, 1)
                    maxima(0, 0)
            pe.wait_ge(s_xT, B)
            pe.wait_ge(s_lo, 2 * B)
            for g in range(4):
                group(0, g, first=True)

            def turn(b, with_experts, last):
                for g in range(4, GB):
                    group(b, g, last)
                if last:
                    with_v(b, GB - 2)
                    with_v(b, GB - 1)
                    output_sums(b, 1)
                    pe.wait_ge(s_dd, d.value())
                    turned(lambda k: attn[:, k, :])
                    project(0)
                    return
                for g in range(4):
                    group(b + 1, g)
                if with_experts:
                    experts(b)

            each_turn(pe, [(d, D_TURN, D_EXPERTS)], turn)


def kernel(L0_attn_x, L0_attn_wq_w, L0_attn_wq_b, L0_attn_wk_w, L0_attn_wk_b, L0_attn_wv_w, L0_attn_wv_b, L0_attn_wo_w,
           L0_attn_wo_b, L0_ffn_gate_w, L0_ffn_c_fc, L0_ffn_fc_bias, L0_ffn_c_proj, L0_ffn_proj_bias):
    import numpy as np
    import concourse.bacc as bacc
    from concourse.bass_utils import run_bass_kernel_spmd

    def turned(w):
        return np.ascontiguousarray(np.asarray(w).T)

    tail = np.zeros((P, 3), np.float32)
    tail[TAIL:TAIL + 2, 0] = 1.0
    tail[TAIL + 2:TAIL + 4, 1] = 1.0
    tail[MASKROW, 2] = 1.0
    keys = np.concatenate([E - np.arange(E), CAP * np.arange(E)]).astype(np.float32)
    ins = {
        "x": np.asarray(L0_attn_x).reshape(N, C),
        "wq": turned(L0_attn_wq_w), "wk": turned(L0_attn_wk_w), "wv": turned(L0_attn_wv_w),
        "gate": np.asarray(L0_ffn_gate_w), "wo": turned(L0_attn_wo_w),
        "bq": np.asarray(L0_attn_wq_b).reshape(C, 1), "bk": np.asarray(L0_attn_wk_b).reshape(C, 1),
        "bv": np.asarray(L0_attn_wv_b).reshape(1, C), "bo": np.asarray(L0_attn_wo_b).reshape(1, C),
        "c_fc": np.asarray(L0_ffn_c_fc),
        "fcb": np.ascontiguousarray(np.asarray(L0_ffn_fc_bias).reshape(E, HC, P).transpose(0, 2, 1)),
        "c_proj": np.asarray(L0_ffn_c_proj), "pjb": np.asarray(L0_ffn_proj_bias),
        "ident": np.eye(P, dtype=np.float32),
        "prefix": np.triu(np.ones((P, P), np.float32), 1),
        "keys": np.tile(keys, (P, 1)),
        "tail": tail,
    }
    nc = bacc.Bacc("TRN2", target_bir_lowering=False, num_devices=1)
    arrays, args = {}, []
    for name, a in ins.items():
        a = np.ascontiguousarray(a)
        arrays[f"in_{name}"] = a
        args.append(nc.dram_tensor(f"in_{name}", a.shape, mybir.dt.from_np(a.dtype), kind="ExternalInput").ap())
    out = nc.dram_tensor("out_0", [N, C], F32, kind="ExternalOutput").ap()
    build(nc, *args, out)
    r = run_bass_kernel_spmd(nc, [arrays], core_ids=[0])
    return r.results[0]["out_0"].reshape(B, T, C)
```

```python
from contextlib import ExitStack

import concourse.bass as bass
from concourse import mybir
from concourse.alu_op_type import AluOpType as ALU

F32 = mybir.dt.float32
F32R = mybir.dt.float32r
I32 = mybir.dt.int32
ACT = mybir.ActivationFunctionType
AX = mybir.AxisListType

P = 128
B, T, C = 8, 512, 128
H, DH = 16, 8
E, TOPK = 8, 2
HID = 4 * C
N = B * T
CAP = int(1.25 * N * TOPK / E)
SLOTS = E * CAP
NT = N // P
TT = T // P
HC = HID // P
ST = CAP // P
SCALE = float(DH) ** -0.5
EPS = 1e-5
MASKED = -float(2 ** 100)
UH = 8
UNITS = H // UH
GROUPS = 2 * TT
GB = UNITS * GROUPS
LEAD = 6
HALVES = 2 * UNITS
ROWS = 4 * DH
TAIL = 2 * ROWS
MASKROW = TAIL + 4
BIGSLOT = 4.0 * SLOTS
CH = [(0, 512), (512, 512), (1024, 256)]
NCH = len(CH)
KN = TOPK * NT
EXPERTS_FROM, EXPERTS_TO = 2, 6
assert 2 * (EXPERTS_TO - EXPERTS_FROM) == E
N_CONST = 13
WR_DMAS, LOAD_DMAS = 5, 8
ZERO_DMAS, ROW_DMAS = 10, 6
D_FIRST = (LEAD + 4) * TT
D_BANK = -D_FIRST % 3
D_TURN = GB * TT + 4
D_EXPERTS = 2 * 2 * NCH
D_EXPERTS_FROM = D_FIRST + EXPERTS_FROM * D_TURN + D_TURN


class Count:

    def __init__(self, base=0):
        self.base, self.local, self.turn, self.per, self.since = base, 0, None, 0, 0

    def enter(self, turn, per):
        self.base, self.local = self.base + self.local, 0
        self.turn, self.per = turn, per
        self.since = 0

    def leave(self, turns):
        assert self.local == self.per, (self.local, self.per)
        self.base, self.local, self.turn = self.base + turns * self.per, 0, None

    def step(self, k=1):
        self.local += k
        self.since += k

    def least(self, k=0):
        return self.base + self.local + k

    def value(self, k=0):
        if self.turn is None:
            return self.least(k)
        return self.turn * self.per + self.least(k)


def build(nc, x, wq, wk, wv, gate, wo, bq, bk, bv, bo, c_fc, fcb, c_proj, pjb, ident_d, prefix_d, keys_d, tail_d, out):
    with ExitStack() as ctx:
        def sb(name, shape, dt=F32):
            return ctx.enter_context(nc.sbuf_tensor(name, shape, dt))

        def ps(name):
            return ctx.enter_context(nc.psum_tensor(name, [P, 512], F32))

        def sem(name):
            return ctx.enter_context(nc.semaphore(name))

        q_parts = nc.dram_tensor("q_parts", [B, C, 2, T], F32, kind="Internal").ap()
        k_parts = nc.dram_tensor("k_parts", [B, 2, C, 2, T], F32, kind="Internal").ap()
        mask_row = nc.dram_tensor("mask_row", [B, T], F32, kind="Internal").ap()
        slot_x = nc.dram_tensor("slot_x", [SLOTS, C], F32, kind="Internal").ap()
        slot_y = nc.dram_tensor("slot_y", [SLOTS, C], F32, kind="Internal").ap()

        ident = sb("ident", [P, P])
        prefix = sb("prefix", [P, P])
        prefix_r = sb("prefix_r", [P, P], F32R)
        ones_r = sb("ones_r", [P, P], F32R)
        ones = sb("ones", [P, P])
        keys = sb("keys", [P, 2 * E])
        wq_s, wk_s, wo_s = sb("wq_s", [C, C]), sb("wk_s", [C, C]), sb("wo_s", [C, C])
        wvg_s = sb("wvg_s", [C, C + E])
        bq_s, bk_s = sb("bq_s", [C, 1]), sb("bk_s", [C, 1])
        bv_s, bo_s = sb("bv_s", [P, C]), sb("bo_s", [P, C])
        acc = sb("acc", [P, NT, C])
        xn_all = sb("xn_all", [P, NT, C])
        v_all = sb("v_all", [P, NT, C])
        K = [sb(f"K{u}", [P, UH, T], F32R) for u in range(UNITS)]
        Q = [sb(f"Q{u}", [P, UH // 2, T], F32R) for u in range(UNITS)]
        total = sb("total", [P, KN, E])
        tail = sb("tail", [5, 2, T])
        zeros4 = sb("zeros4", [4, 2, T], F32R)
        probs = sb("probs", [P, 8, T])
        v_aug = sb("v_aug", [P, TT, H, 32])
        nmax = [sb(f"nmax{q}", [P, TT, 4]) for q in range(2)]
        nmhl = [sb(f"nmhl{q}", [P, TT, 4, 2], F32R) for q in range(2)]
        nmT = [sb(f"nmT{q}", [8, T], F32R) for q in range(2)]
        pv_s = sb("pv_s", [P, T])
        rsum = sb("rsum", [P, TT, 4, 2])
        attn = sb("attn", [P, TT, C])
        attnT = sb("attnT", [C, T])
        hid = sb("hid", [P, HC, CAP])
        xe = sb("xe", [P, ST, C])
        xeT = sb("xeT", [C, CAP])
        ye = sb("ye", [P, ST, C])
        wfc = [sb(f"wfc{q}", [C, HID]) for q in range(2)]
        wpj = [sb(f"wpj{q}", [P, HC, C]) for q in range(2)]
        fcb_s = [sb(f"fcb{q}", [P, HC]) for q in range(2)]
        pjb_s = [sb(f"pjb{q}", [P, C]) for q in range(2)]
        hid_f = hid[:, :, :].rearrange("p a b -> p (a b)")
        parts = {(w, q): hid_f[:, (2 * w + q) * 2 * T:(2 * w + q + 1) * 2 * T].rearrange("p (s t) -> p s t", s=2)
                 for w in range(2) for q in range(2)}
        xst = [xe[:, TT * q:TT * (q + 1), :] for q in range(2)]
        xT = [xeT[:, T * q:T * (q + 1)] for q in range(2)]
        stats = [sb(f"stats{q}", [P, TT, 6]) for q in range(2)]
        mv = [sb(f"mv{q}", [P, TT, 2]) for q in range(2)]
        var = [sb(f"var{q}", [P, TT]) for q in range(2)]
        std = [sb(f"std{q}", [P, TT]) for q in range(2)]
        rstd = [sb(f"rstd{q}", [P, TT]) for q in range(2)]
        mrow = [sb(f"mrow{q}", [1, T], F32R) for q in range(2)]
        logit = sb("logit", [P, NT, E])
        r_eq = sb("r_eq", [P, NT, E])
        r_key = sb("r_key", [P, NT, E])
        top = sb("top", [P, TOPK, NT])
        kmax = sb("kmax", [P, NT])
        hot = sb("hot", [P, KN, E], F32R)
        scan = sb("scan", [P, KN, E])
        rank = sb("rank", [P, KN, E])
        keep = sb("keep", [P, KN])
        gap = sb("gap", [P, NT])
        prob = sb("prob", [P, KN])
        wgt = sb("wgt", [P, KN])
        slot_f = sb("slot_f", [P, KN])
        put_f = sb("put_f", [P, KN])
        put_i = sb("put_i", [P, KN], I32)
        get_i = sb("get_i", [P, KN], I32)

        bA = [ps(f"bA{n}") for n in range(4)]
        bD = [ps(f"bD{n}") for n in range(3)]
        bPV = ps("bPV")

        s_const = sem("s_const")
        s_fill = sem("s_fill")
        s_rows = sem("s_rows")
        s_xin = [sem("s_xin0"), sem("s_xin1")]
        s_var = sem("s_var")
        s_std = sem("s_std")
        s_xn = sem("s_xn")
        s_tp = sem("s_tp")
        s_copy = sem("s_copy")
        s_bo = sem("s_bo")
        s_xT = sem("s_xT")
        s_qk = sem("s_qk")
        s_hi = sem("s_hi")
        s_lo = sem("s_lo")
        s_vg = sem("s_vg")
        s_ve = sem("s_ve")
        s_mask = sem("s_mask")
        s_wr = [sem("s_wr0"), sem("s_wr1")]
        s_hot = sem("s_hot")
        s_rank = sem("s_rank")
        s_gap = sem("s_gap")
        s_gexp = sem("s_gexp")
        s_ranks = sem("s_ranks")
        s_scan = sem("s_scan")
        s_prob = sem("s_prob")
        s_slots = sem("s_slots")
        s_put = sem("s_put")
        s_chain = sem("s_chain")
        s_load = [[sem(f"s_load{u}{q}") for q in range(2)] for u in range(UNITS)]
        s_st = sem("s_st")
        s_exp = sem("s_exp")
        s_pv = sem("s_pv")
        s_pvo = sem("s_pvo")
        s_d = sem("s_d")
        s_dd = sem("s_dd")
        s_nm = sem("s_nm")
        s_nt = sem("s_nt")
        s_ne = sem("s_ne")
        s_nq = [sem("s_nq0"), sem("s_nq1")]
        s_vaug = sem("s_vaug")
        s_w = [sem("s_w0"), sem("s_w1")]
        s_xe = sem("s_xe")
        s_up = sem("s_up")
        s_ge = sem("s_ge")
        s_zero = sem("s_zero")
        s_slot = sem("s_slot")
        s_get = [sem(f"s_get{b}") for b in range(B)]
        s_comb = sem("s_comb")
        s_out = sem("s_out")

        x_v = x.rearrange("(n p) c -> p n c", p=P)
        out_v = out.rearrange("(n p) c -> p n c", p=P)
        slot_x_v = slot_x.rearrange("(e s p) c -> e p s c", s=ST, p=P)
        slot_y_v = slot_y.rearrange("(e s p) c -> e p s c", s=ST, p=P)

        def rows(t, b, k=0, n=TT):
            return t[:, bass.ds(b * TT + k, n), :]

        def wait(eng, s, value):
            if not isinstance(value, int) or value > 0:
                eng.wait_ge(s, value)

        def each_batch(eng, step):
            for q in range(2):
                step(q, q)
            with eng.Fori(1, B // 2) as i:
                for q in range(2):
                    step(i * 2 + q, q)

        def each_turn(eng, counts, turn):
            for start, end, experts in ((0, EXPERTS_FROM, False), (EXPERTS_FROM, EXPERTS_TO, True)):
                with eng.Fori(start, end) as b:
                    for c, per, more in counts:
                        c.enter(b - start if start else b, per + more * experts)
                    turn(b, experts, False)
                for c, _, _ in counts:
                    c.leave(end - start)
            for b in range(EXPERTS_TO, B):
                for c, _, _ in counts:
                    c.since = 0
                turn(b, False, b == B - 1)

        def gathered(b, n):
            n += (b % 4) * TOPK * TT
            return xn_all[:, n, :] if b < 4 else hid_f[:, n * C:(n + 1) * C]

        block = ctx.enter_context(nc.Block())

        @block.sync
        def _(sp):
            def load_x(b, q):
                sp.dma_start(rows(acc, b), rows(x_v, b)).then_inc(s_xin[q], 16)

            load_x(0, 0)
            load_x(1, 1)
            for t, src in ((ident, ident_d), (wq_s, wq), (bq_s, bq), (wk_s, wk), (bk_s, bk)):
                sp.dma_start(t[:], src).then_inc(s_const, 16)
            sp.dma_start(wvg_s[:, 0:C], wv).then_inc(s_const, 16)
            sp.dma_start(wvg_s[:, C:C + E], gate).then_inc(s_const, 16)
            sp.dma_start(bv_s[:], bv.to_broadcast([P, C])).then_inc(s_const, 16)
            sp.dma_start(bo_s[:], bo.to_broadcast([P, C])).then_inc(s_const, 16)
            for t, src in ((tail, tail_d), (prefix, prefix_d), (keys, keys_d), (wo_s, wo)):
                sp.dma_start(t[:], src).then_inc(s_const, 16)

            def write_stacks(b, q):
                sp.wait_ge(s_lo, b * 2 + 2)
                sp.dma_start(q_parts[b], parts[0, q]).then_inc(s_wr[q], 16)
                sp.dma_start(k_parts[b][0], parts[1, q]).then_inc(s_wr[q], 16)
                for s in range(2):
                    sp.dma_start(k_parts[b][1, :, s:s + 1, :], parts[1, q][:, 1 - s:2 - s, :]).then_inc(s_wr[q], 16)
                sp.wait_ge(s_mask, b + 1)
                sp.dma_start(mask_row[bass.ds(b, 1), :], mrow[q][:].bitcast(F32)).then_inc(s_wr[q], 16)

            def step(b, q):
                sp.wait_ge(s_xn, b + 1)
                load_x(b + 2, q)
                if not isinstance(b, int) or b > 0:
                    write_stacks(b - 1, 1 - q)

            step(0, 0)
            with sp.Fori(0, B // 2 - 2) as i:
                for q in range(2):
                    step(i * 2 + q + 1, 1 - q)
            step(B - 3, 1)
            write_stacks(B - 3, 1)

            def load_quad(b, u, q):
                pair0 = u * (UH // 2) + 2 * q
                qs = q_parts[b].rearrange("(pair c) s t -> (c s) pair t", c=2 * DH)
                ks = k_parts[b].rearrange("r (pair e c) s t -> r e (c s) pair t", e=2, c=DH)
                kd = K[u][:, 4 * q:4 * q + 4, :].bitcast(F32).rearrange("p (pair e) t -> p e pair t", e=2)
                for r in range(2):
                    at = r * ROWS
                    sp.dma_start(Q[u][at:at + ROWS, 2 * q:2 * q + 2, :].bitcast(F32), qs[:, pair0:pair0 + 2, :]
                                 ).then_inc(s_load[u][q], 16)
                    for e in range(2):
                        row = at + e * 2 * DH
                        sp.dma_start(kd[row:row + 2 * DH, e, :, :], ks[r, e, :, pair0:pair0 + 2, :]
                                     ).then_inc(s_load[u][q], 16)
                sp.dma_start(K[u][MASKROW:MASKROW + 1, 4 * q:4 * q + 4, :].bitcast(F32),
                             mask_row[bass.ds(b, 1), None, :].to_broadcast([1, 4, T])).then_inc(s_load[u][q], 16)
                sp.dma_start(Q[u][TAIL:TAIL + 4, 2 * q:2 * q + 2, :].bitcast(F32), zeros4[:].bitcast(F32)).then_inc(s_load[u][q], 16)

            def max_rows(u, q, m):
                sp.wait_ge(s_ne, m + 1)
                for pair in range(2):
                    sp.dma_start(Q[u][TAIL:TAIL + 4, 2 * q + pair, :].bitcast(F32),
                                 nmT[q][4 * pair:4 * pair + 4, :].bitcast(F32)).then_inc(s_nq[q], 16)

            sp.wait_ge(s_rows, ROW_DMAS * 16)
            for q in range(2):
                sp.wait_ge(s_wr[q], (B // 2 - 1) * WR_DMAS * 16)
            for q in range(2):
                load_quad(0, 0, q)
            write_stacks(B - 2, 0)
            for q in range(2):
                load_quad(0, 1, q)
            write_stacks(B - 1, 1)
            for q in range(2):
                max_rows(0, q, q)
            for q in range(2):
                sp.wait_ge(s_wr[q], B // 2 * WR_DMAS * 16)

            def load_rows(e):
                sp.dma_start(xe[:], slot_x_v[e]).then_inc(s_xe, 16)

            def load_experts(b):
                e = b * 2 - 2 * EXPERTS_FROM
                sp.wait_ge(s_put, KN * 16)
                load_rows(e)
                for q in range(2):
                    sp.dma_start(wfc[q][:], c_fc[e + q]).then_inc(s_w[q], 16)
                    sp.dma_start(wpj[q][:], c_pj_v[e + q]).then_inc(s_w[q], 16)
                    sp.dma_start(fcb_s[q][:], fcb[e + q]).then_inc(s_w[q], 16)
                    sp.dma_start(pjb_s[q][:], pjb[e + q].to_broadcast([P, C])).then_inc(s_w[q], 16)

            def experts(b):
                for q in range(2):
                    e = b * 2 - 2 * EXPERTS_FROM + q
                    before = (b - EXPERTS_FROM) * (D_TURN + D_EXPERTS) + D_EXPERTS_FROM + q * 2 * NCH
                    if q == 0:
                        sp.wait_ge(s_dd, before + NCH)
                        load_rows(e + 1)
                    sp.wait_ge(s_dd, before + 2 * NCH)
                    sp.dma_start(slot_y_v[e], ye[:]).then_inc(s_slot, 16)

            c_pj_v = c_proj.rearrange("e (h p) c -> e p h c", p=P)

            def turn(b, with_experts, last):
                if with_experts:
                    load_experts(b)
                through = b * (4 * GB)
                m = b * HALVES + 2
                max_rows(1, 0, m)
                if last:
                    max_rows(1, 1, m + 1)
                    return
                sp.wait_ge(s_st, through + 4 * 4)
                load_quad(b + 1, 0, 0)
                sp.wait_ge(s_st, through + 4 * 8)
                load_quad(b + 1, 0, 1)
                max_rows(1, 1, m + 1)
                sp.wait_ge(s_st, through + 4 * 12)
                load_quad(b + 1, 1, 0)
                max_rows(0, 0, m + 2)
                sp.wait_ge(s_st, through + 4 * 16)
                load_quad(b + 1, 1, 1)
                max_rows(0, 1, m + 3)
                if with_experts:
                    experts(b)

            each_turn(sp, [], turn)
            for b in range(B):
                sp.wait_ge(s_comb, b + 1)
                sp.dma_start(rows(out_v, b), rows(acc, b)).then_inc(s_out, 16)
            sp.wait_ge(s_out, B * 16)

        @block.gpsimd
        def _(pool):
            for t in (K[0], K[1], Q[0], Q[1], zeros4):
                nc.gpsimd.memset(t[:].bitcast(F32), 0.0).then_inc(s_fill, 1)
            pool.wait_ge(s_fill, 5)
            pool.wait_ge(s_const, N_CONST * 16)
            for u in range(UNITS):
                kt = K[u][TAIL:TAIL + 4, :, :].bitcast(F32).rearrange("p (pair e) t -> p e pair t", e=2)
                for e in range(2):
                    pool.dma_start(kt[:, e], tail[0:4, e:e + 1, :].to_broadcast([4, UH // 2, T])).then_inc(s_rows, 16)
                pool.dma_start(Q[u][MASKROW:MASKROW + 1, :, :].bitcast(F32),
                               tail[4:5, 0:1, :].to_broadcast([1, UH // 2, T])).then_inc(s_rows, 16)

            def front(b, q):
                pool.wait_ge(s_xn, b + 1)
                pool.wait_ge(s_xT, b + 1)
                wait(pool, s_wr[q], (b - q) * (WR_DMAS * 16 // 2))
                if not isinstance(b, int) or b > 0:
                    add_bv(b - 1)
                nc.gpsimd.tensor_scalar(mrow[q][:], xT[q][0:1, :], 0.0, MASKED, ALU.is_equal, ALU.mult).then_inc(s_mask, 1)

            def add_bv(b):
                pool.wait_ge(s_ve, b * 2 + 2)
                nc.gpsimd.tensor_tensor(rows(v_all, b), rows(v_all, b), bv_s[:, None, :].to_broadcast([P, TT, C]), ALU.add)

            each_batch(pool, front)
            add_bv(B - 1)
            nc.gpsimd.memset(v_aug[:], 0.0).then_inc(s_fill, 1)
            pool.wait_ge(s_fill, 6)
            for q in range(2):
                va = v_aug[:].rearrange("p j (u r) c -> p (j u) r c", u=UNITS)
                nc.gpsimd.memset(va[:, :, 4 * q:4 * q + 4, 16 + q], 1.0).then_inc(s_fill, 1)

            steps = [0]

            def link(ins):
                ins.then_inc(s_slots, 1)
                steps[0] += 1
                pool.wait_ge(s_slots, steps[0])

            pool.wait_ge(s_ranks, 1)
            pool.wait_ge(s_scan, 1)
            flat = [t.rearrange("p n e -> p (n e)") for t in (scan[:], total[:], rank[:], hot[:].bitcast(F32))]
            link(nc.gpsimd.tensor_tensor(flat[0], flat[0], flat[1], ALU.subtract))
            link(nc.gpsimd.tensor_tensor(flat[2], flat[0], flat[2], ALU.add))
            nc.gpsimd.tensor_tensor(scan[:], hot[:].bitcast(F32), keys[:, None, E:2 * E].to_broadcast([P, KN, E]), ALU.mult)
            link(nc.gpsimd.tensor_tensor(flat[2], flat[2], flat[3], ALU.mult))
            for half in (4, 2, 1):
                nc.gpsimd.tensor_tensor(rank[:, :, 0:half], rank[:, :, 0:half], rank[:, :, half:2 * half], ALU.add)
                link(nc.gpsimd.tensor_tensor(scan[:, :, 0:half], scan[:, :, 0:half], scan[:, :, half:2 * half], ALU.add))
            r_at, r_base = rank[:, :, 0], scan[:, :, 0]
            link(nc.gpsimd.tensor_scalar(keep[:], r_at, float(CAP), None, ALU.is_lt))
            link(nc.gpsimd.tensor_tensor(slot_f[:], r_at, keep[:], ALU.mult))
            link(nc.gpsimd.tensor_tensor(slot_f[:], slot_f[:], r_base, ALU.add))
            nc.gpsimd.tensor_copy(get_i[:], slot_f[:])
            link(nc.gpsimd.tensor_scalar(put_f[:], keep[:], -BIGSLOT, BIGSLOT, ALU.mult, ALU.add))
            link(nc.gpsimd.tensor_tensor(put_f[:], put_f[:], slot_f[:], ALU.add))
            pool.wait_ge(s_prob, 1)
            nc.gpsimd.tensor_tensor(wgt[:], prob[:], keep[:], ALU.mult)
            link(nc.gpsimd.tensor_copy(put_i[:], put_f[:]))

            for q in range(2):
                pool.wait_ge(s_wr[q], B // 2 * WR_DMAS * 16)
            per = SLOTS * C // P // ZERO_DMAS
            nc.gpsimd.memset(hid_f[:, 0:per], 0.0).then_inc(s_fill, 1)
            pool.wait_ge(s_fill, 9)
            pool.wait_ge(s_nq[0], 32)
            for h in range(ZERO_DMAS):
                pool.dma_start(slot_x.rearrange("(p h r) c -> h p (r c)", p=P, h=ZERO_DMAS)[h], hid_f[:, 0:per]
                               ).then_inc(s_zero, 16)
                pool.wait_ge(s_zero, h * 16 + 16)
            nc.gpsimd.tensor_tensor(acc[:], acc[:], bo_s[:, None, :].to_broadcast([P, NT, C]), ALU.add).then_inc(s_bo, 1)
            pool.wait_ge(s_copy, B)
            for k in range(TOPK):
                for n in range(NT):
                    col = k * NT + n
                    pool.indirect_dma_start(slot_x, bass.IndirectOffsetOnAxis(ap=put_i[:, col:col + 1], axis=0),
                                            xn_all[:, n, :], None, bounds_check=SLOTS - 1, oob_is_err=False
                                            ).then_inc(s_put, 16)
            pool.wait_ge(s_slot, E * 16 + 16)
            for b in range(B):
                for k in range(TOPK):
                    for n in range(TT):
                        col = k * NT + b * TT + n
                        pool.indirect_dma_start(gathered(b, k * TT + n), None, slot_y,
                                                bass.IndirectOffsetOnAxis(ap=get_i[:, col:col + 1], axis=0),
                                                bounds_check=SLOTS - 1, oob_is_err=False).then_inc(s_get[b], 16)
            for b in range(B):
                pool.wait_ge(s_get[b], TOPK * TT * 16)

        @block.scalar
        def _(act):
            def high(b, q):
                wait(act, s_wr[q], (b - q) * (WR_DMAS * 16 // 2))
                for w, bias in ((0, bq_s), (1, bk_s)):
                    act.wait_ge(s_qk, b * 2 + w + 1)
                    nc.scalar.activation(parts[w, q][:, 0, :].bitcast(F32R), bA[2 + w][:], ACT.Identity, bias=bias[:]
                                         ).then_inc(s_hi, 1)

            def values(b):
                for h in range(2):
                    act.wait_ge(s_vg, b * 2 + h + 1)
                    pv = bD[h][:, 0:2 * (C + E)].rearrange("p (n c) -> p n c", n=2)
                    nc.scalar.copy(rows(v_all, b, 2 * h, 2), pv[:, :, 0:C])
                    nc.scalar.copy(rows(logit, b, 2 * h, 2), pv[:, :, C:C + E]).then_inc(s_ve, 1)

            def front(b, q):
                act.wait_ge(s_var, b + 1)
                nc.scalar.activation(std[q][:], var[q][:], ACT.Sqrt).then_inc(s_std, 1)
                if not isinstance(b, int) or b > 0:
                    high(b - 1, 1 - q)
                    values(b - 1)
                act.wait_ge(s_tp, b + 1)
                wait(act, s_vg, (b - 1) * 2)
                wait(act, s_mask, b - 1)
                nc.scalar.copy(xT[q], bA[q][:]).then_inc(s_xT, 1)
                nc.scalar.copy(rows(xn_all, b), xst[q]).then_inc(s_copy, 1)

            each_batch(act, front)
            high(B - 1, 1)
            values(B - 1)
            act.wait_ge(s_gap, 1)
            nc.scalar.activation(gap[:], gap[:], ACT.Exp).then_inc(s_gexp, 1)
            act.wait_ge(s_rank, 1)
            nc.scalar.copy(rank[:].rearrange("p n e -> p (n e)"), bD[2][:])
            nc.scalar.copy(total[:].rearrange("p n e -> p (n e)"), bPV[:]).then_inc(s_ranks, 1)

            def maxima(m, q, k):
                act.wait_ge(s_nt, m + 1)
                wait(act, s_nq[q], k * 32)
                nc.scalar.copy(nmT[q][:], bA[0][0:8, :]).then_inc(s_ne, 1)

            def group(b, g, last=False, first=False):
                n = b * GB + g
                if g % 4 == 2 and not (last and g // 4 == 3):
                    maxima(b * HALVES + g // 4 + 1, (g // 4 + 1) % 2, b * 2 + (g // 4 + 1) // 2)
                if g == 1 and not first:
                    sums(b * UNITS - 1)
                if g == GROUPS + 1:
                    sums(b * UNITS)
                if g == 1:
                    fill_v(b)
                for h in range(4):
                    act.wait_ge(s_st, n * 4 + h + 1)
                    if h == 0:
                        wait(act, s_pv, n - 1)
                    nc.scalar.activation(probs[:, (g % 2) * 4 + h, :], bA[h][:], ACT.Exp, scale=SCALE).then_inc(s_exp, 1)

            def fill_v(b):
                wait(act, s_pv, b * GB)
                if isinstance(b, int) and b == 0:
                    act.wait_ge(s_fill, 8)
                va = v_aug[:].rearrange("p j (u r) c -> p (j u) r c", u=UNITS)
                vs = rows(v_all, b).rearrange("p j (u r c) -> p (j u) r c", u=UNITS, c=DH)
                for q in range(2):
                    last = nc.scalar.copy(va[:, :, 4 * q:4 * q + 4, DH * q:DH * (q + 1)], vs[:, :, 4 * q:4 * q + 4, :])
                last.then_inc(s_vaug, 1)

            def sums(unit):
                act.wait_ge(s_pv, (unit + 1) * GROUPS)
                nc.scalar.copy(pv_s[:], bPV[:]).then_inc(s_pvo, 1)

            def experts(b):
                for q in range(2):
                    e = b * 2 - 2 * EXPERTS_FROM + q
                    for hc in range(HC):
                        for c, (c0, w) in enumerate(CH):
                            k = hc * NCH + c
                            act.wait_ge(s_up, e * (HC * NCH) + k + 1)
                            nc.scalar.activation(hid[:, hc, c0:c0 + w], bA[k % 4][:, 0:w], ACT.Gelu,
                                                 bias=fcb_s[q][:, hc:hc + 1]).then_inc(s_ge, 1)

            maxima(0, 0, 0)
            for g in range(4):
                group(0, g, first=True)

            def turn(b, with_experts, last):
                for g in range(4, GB):
                    group(b, g, last)
                if last:
                    sums(b * UNITS + 1)
                    return
                for g in range(4):
                    group(b + 1, g)
                if with_experts:
                    experts(b)

            each_turn(act, [], turn)

        @block.vector
        def _(dve):
            chain = [0]

            def link(ins):
                ins.then_inc(s_chain, 1)
                chain[0] += 1
                dve.wait_ge(s_chain, chain[0])

            F = 3

            def norm(b, q):
                dve.wait_ge(s_xin[q], (b - q) * 8 + 16)
                for k in range(TT):
                    last = nc.vector.bn_stats(stats[q][:, k, :], rows(acc, b, k, 1).rearrange("p n c -> p (n c)"))
                last.then_inc(s_chain, 1)
                dve.wait_ge(s_chain, b * F + 1)
                nc.vector.memset(var[q][:], 0.0)
                for k in range(TT):
                    last = nc.vector.bn_aggr(mv[q][:, k, :], stats[q][:, k, :])
                last.then_inc(s_chain, 1)
                dve.wait_ge(s_chain, b * F + 2)
                nc.vector.tensor_scalar(var[q][:], mv[q][:, :, 1], EPS, None, ALU.add).then_inc(s_var, 1)
                dve.wait_ge(s_std, b + 1)
                nc.vector.reciprocal(rstd[q][:], std[q][:]).then_inc(s_chain, 1)
                dve.wait_ge(s_chain, b * F + 3)
                wait(dve, s_tp, b - 1)
                wait(dve, s_copy, b - 1)
                for k in range(TT):
                    last = nc.vector.tensor_scalar(xst[q][:, k, :], rows(acc, b, k, 1).rearrange("p n c -> p (n c)"),
                                                   mv[q][:, k, 0:1], rstd[q][:, k:k + 1], ALU.subtract, ALU.mult)
                last.then_inc(s_xn, 1)

            def late(b, q):
                for w, bias in ((0, bq_s), (1, bk_s)):
                    dve.wait_ge(s_hi, b * 2 + w + 1)
                    nc.vector.scalar_tensor_tensor(out=parts[w, q][:, 1, :].bitcast(F32R), in0=bA[2 + w][:], scalar=bias[:],
                                                   in1=parts[w, q][:, 0, :], op0=ALU.add, op1=ALU.subtract).then_inc(s_lo, 1)
            def front(b, q):
                norm(b, q)
                if not isinstance(b, int) or b > 0:
                    late(b - 1, 1 - q)

            nc.vector.memset(ones[:], 1.0).then_inc(s_slot, 16)
            each_batch(dve, front)
            late(B - 1, 1)
            chain[0] = B * F
            dve.wait_ge(s_const, N_CONST * 16)

            nc.vector.tensor_copy(prefix_r[:], prefix[:])
            nc.vector.tensor_copy(ones_r[:], ones[:])
            lg = logit[:]
            hot_k = hot[:].rearrange("p (k n) e -> p k n e", k=TOPK)
            wide = [P, NT, E]
            dve.wait_ge(s_ve, 2 * B)
            for k in range(TOPK):
                link(nc.vector.tensor_reduce(top[:, k, :], lg, AX.X, ALU.max))
                link(nc.vector.tensor_tensor(r_eq[:], lg, top[:, k, :, None].to_broadcast(wide), ALU.is_equal))
                link(nc.vector.tensor_tensor(r_key[:], r_eq[:], keys[:, None, 0:E].to_broadcast(wide), ALU.mult))
                link(nc.vector.tensor_reduce(kmax[:], r_key[:], AX.X, ALU.max))
                ins = nc.vector.tensor_tensor(hot_k[:, k], r_key[:], kmax[:, :, None].to_broadcast(wide), ALU.is_equal)
                if k == TOPK - 1:
                    ins.then_inc(s_hot, 1)
                else:
                    link(ins)
                    link(nc.vector.scalar_tensor_tensor(out=lg, in0=hot_k[:, k].bitcast(F32), scalar=MASKED, in1=lg, op0=ALU.mult,
                                                        op1=ALU.add))
            nc.vector.tensor_tensor(gap[:], top[:, 1, :], top[:, 0, :], ALU.subtract).then_inc(s_gap, 1)
            dve.wait_ge(s_gexp, 1)
            link(nc.vector.tensor_scalar(kmax[:], gap[:], 1.0, None, ALU.add))
            link(nc.vector.reciprocal(prob[:, 0:NT], kmax[:]))
            nc.vector.tensor_tensor(prob[:, NT:KN], prob[:, 0:NT], gap[:], ALU.mult).then_inc(s_prob, 1)
            dve.wait_ge(s_ranks, 1)
            for e in range(E):
                last = nc.vector.tensor_tensor_scan(scan[:, :, e], ones[:, 0:KN], total[:, :, e], 0.0, ALU.mult, ALU.add)
            last.then_inc(s_scan, 1)

            d = Count()
            d.since = D_BANK
            own = Count()
            own.step(chain[0])

            def chained(ins):
                ins.then_inc(s_chain, 1)
                own.step()
                dve.wait_ge(s_chain, own.value())

            def bank():
                return bD[d.since % 3]

            def take():
                dve.wait_ge(s_d, d.value(1))

            def scores_max(s):
                q, head = (s // 4) % 2, s % 4
                for k in range(TT):
                    take()
                    nc.vector.tensor_reduce(nmax[q][:, k, head:head + 1], bank()[:], AX.X, ALU.max, negate=True
                                            ).then_inc(s_dd, 1)
                    d.step()
                if head == 3:
                    dve.wait_ge(s_dd, d.value())
                    chained(nc.vector.tensor_copy(nmhl[q][:, :, :, 0], nmax[q][:]))
                    nc.vector.tensor_tensor(nmhl[q][:, :, :, 1], nmax[q][:], nmhl[q][:, :, :, 0].bitcast(F32), ALU.subtract
                                            ).then_inc(s_nm, 1)

            def normalise(u):
                take()
                src = bank()[:].rearrange("p (k c) -> p k c", c=P)
                sums = bank()[:].rearrange("p (kg c) -> p kg c", c=32)[:, :, 2 * DH:2 * DH + 2]
                chained(nc.vector.reciprocal(rsum[:].rearrange("p k g q -> p (k g) q"), sums))
                for q in range(2):
                    o = attn[:, :, u * 64 + q * 32:u * 64 + (q + 1) * 32].rearrange("p k (g c) -> p k g c", c=DH)
                    i0 = src.rearrange("p k (g c) -> p k g c", c=32)[:, :, :, DH * q:DH * (q + 1)]
                    last = nc.vector.tensor_tensor(o, i0, rsum[:, :, :, q:q + 1].to_broadcast([P, TT, 4, DH]), ALU.mult)
                last.then_inc(s_dd, 1)
                d.step()

            def take_attnT():
                take()
                nc.vector.tensor_copy(attnT[:], bank()[:]).then_inc(s_dd, 1)
                d.step()

            def take_out(b, done=s_dd):
                dve.wait_ge(s_bo, 1)
                take()
                nc.vector.tensor_tensor(rows(acc, b), bank()[:].rearrange("p (k c) -> p k c", c=C), rows(acc, b), ALU.add
                                        ).then_inc(done, 1)
                d.step()

            def experts(b):
                for q in range(2):
                    e = b * 2 - 2 * EXPERTS_FROM + q
                    for (c0, w) in CH:
                        take()
                        nc.vector.tensor_copy(xeT[:, c0:c0 + w], bank()[:, 0:w]).then_inc(s_dd, 1)
                        d.step()
                    dve.wait_ge(s_slot, e * 16 + 16)
                    for (c0, w) in CH:
                        take()
                        k0, nk = c0 // P, w // P
                        nc.vector.tensor_tensor(ye[:, k0:k0 + nk, :], bank()[:, 0:w].rearrange("p (k c) -> p k c", c=C),
                                                pjb_s[q][:, None, :].to_broadcast([P, nk, C]), ALU.add).then_inc(s_dd, 1)
                        d.step()

            def combine(b):
                dve.wait_ge(s_get[b], TOPK * TT * 16)
                for k in range(TOPK):
                    for n in range(TT):
                        t, col = b * TT + n, k * NT + b * TT + n
                        last = nc.vector.scalar_tensor_tensor(out=acc[:, t, :], in0=gathered(b, k * TT + n),
                                                              scalar=wgt[:, col:col + 1], in1=acc[:, t, :], op0=ALU.mult,
                                                              op1=ALU.add)
                    if k == 0 or b == B - 1:
                        chained(last)
                if b == B - 1:
                    return
                last.then_inc(s_comb, 1)


            def group(b, g, last=False, first=False):
                if not last or g + LEAD < GB:
                    scores_max((g + LEAD) % UH)
                if g == 1 and not first:
                    normalise(1)
                if g == 2 and not first:
                    take_attnT()
                if g == 3 and not first:
                    take_out(b - 1)
                if g == GROUPS + 1:
                    normalise(0)

            for s in range(LEAD):
                scores_max(s)
            for g in range(4):
                group(0, g, first=True)

            def turn(b, with_experts, last):
                for g in range(4, GB):
                    group(b, g, last)
                    if last and g >= GB - B:
                        combine(g - (GB - B))
                if last:
                    normalise(1)
                    take_attnT()
                    take_out(b, s_comb)
                    return
                for g in range(4):
                    group(b + 1, g)
                if with_experts:
                    experts(b)

            each_turn(dve, [(d, D_TURN, D_EXPERTS), (own, HALVES + UNITS, 0)], turn)
        @block.tensor
        def _(pe):
            def products(b, q):
                pe.wait_ge(s_xT, b + 1)
                for w, weights in ((0, wq_s), (1, wk_s)):
                    wait(pe, s_lo, b * 2 - 1 + w)
                    nc.tensor.matmul(bA[2 + w][:], weights[:], xT[q], start=True, stop=True).then_inc(s_qk, 1)
                for h in range(2):
                    wait(pe, s_ve, b * 2 - 1 + h)
                    for n in range(2):
                        k = 2 * h + n
                        last = nc.tensor.matmul(bD[h][:, n * (C + E):(n + 1) * (C + E)], xT[q][:, k * P:(k + 1) * P], wvg_s[:],
                                                start=True, stop=True)
                    last.then_inc(s_vg, 1)

            def front(b, q):
                if not isinstance(b, int) or b > 0:
                    products(b - 1, 1 - q)
                pe.wait_ge(s_xn, b + 1)
                wait(pe, s_xT, b - 1)
                for k in range(TT):
                    last = nc.tensor.transpose(bA[q][:, k * P:(k + 1) * P], xst[q][:, k, :], ident[:])
                last.then_inc(s_tp, 1)

            pe.wait_ge(s_const, N_CONST * 16)
            each_batch(pe, front)
            products(B - 1, 1)

            pe.wait_ge(s_hot, 1)
            hot_f = hot[:].rearrange("p n e -> p (n e)")
            nc.tensor.matmul(bD[2][:], prefix_r[:], hot_f, start=True, stop=True)
            nc.tensor.matmul(bPV[:], ones_r[:], hot_f, start=True, stop=True).then_inc(s_rank, 1)

            d = Count()
            d.since = D_BANK

            def free():
                if d.turn is not None or d.least() > 2:
                    pe.wait_ge(s_dd, d.value(-1 if d.since < 2 else -2))
                return bD[d.since % 3]

            def done(ins):
                ins.then_inc(s_d, 1)
                d.step()

            def scores_for_max(b, u, s, first, n):
                q = s // 4
                if s % 4 == 0 and first == 0:
                    pe.wait_ge(s_load[u][q], b * (LOAD_DMAS * 16) + LOAD_DMAS * 16)
                for k in range(first, first + n):
                    done(nc.tensor.matmul(free()[:], Q[u][:, s // 2, k * P:(k + 1) * P], K[u][:, s, :], start=True, stop=True))

            def maxima(m, q, n=None):
                pe.wait_ge(s_nm, m + 1)
                if n is not None:
                    pe.wait_ge(s_exp, n * 4 - 3)
                for k in range(TT):
                    last = nc.tensor.transpose(bA[0][0:8, k * P:(k + 1) * P],
                                               nmhl[q][:, k, :, :].rearrange("p h s -> p (h s)").bitcast(F32), ident[:])
                last.then_inc(s_nt, 1)

            def scores(b, g, first, n, new_maxima=False):
                u, q, j = g // GROUPS, (g % GROUPS) // 4, g % 4
                if j == 0 and first == 0:
                    pe.wait_ge(s_nq[q], (b * UNITS + u) * 32 + 32)
                for h in range(first, first + n):
                    if h == 0 and new_maxima:
                        pe.wait_ge(s_ne, b * HALVES + g // 4 + 2)
                    else:
                        wait(pe, s_exp, (b * GB + g) * 4 - 3 + h)
                    nc.tensor.matmul(bA[h][:], K[u][:, 4 * q + h, j * P:(j + 1) * P], Q[u][:, 2 * q + h // 2, :],
                                     start=True, stop=True).then_inc(s_st, 1)

            def with_v(b, g):
                n = b * GB + g
                u, q, j = g // GROUPS, (g % GROUPS) // 4, g % 4
                pe.wait_ge(s_exp, n * 4 + 4)
                if g == 0:
                    pe.wait_ge(s_vaug, b + 1)
                if g % GROUPS == 0:
                    wait(pe, s_pvo, b * UNITS + u)
                for h in range(4):
                    last = nc.tensor.matmul(bPV[32 * h:32 * h + 32, :], v_aug[:, j, u * UH + 4 * q + h, :],
                                            probs[:, (g % 2) * 4 + h, :], start=(g % GROUPS == 0),
                                            stop=(g % GROUPS == GROUPS - 1))
                last.then_inc(s_pv, 1)

            def turned(src, n=TT):
                to = free()
                for k in range(n):
                    last = nc.tensor.transpose(to[:, k * P:(k + 1) * P], src(k), ident[:])
                done(last)

            def output_sums(b, u):
                pe.wait_ge(s_pvo, b * UNITS + u + 1)
                turned(lambda k: pv_s[:, k * P:(k + 1) * P])

            def project(since=TT):
                pe.wait_ge(s_dd, d.value(-since))
                to = free()
                for k in range(TT):
                    last = nc.tensor.matmul(to[:, k * P:(k + 1) * P], attnT[:, k * P:(k + 1) * P], wo_s[:], start=True,
                                            stop=True)
                done(last)

            def attn_turned():
                pe.wait_ge(s_dd, d.value(-TT))
                turned(lambda k: attn[:, k, :])

            def group(b, g, last=False, first=False):
                def ahead(k, n):
                    head = g + LEAD
                    if head < GB:
                        scores_for_max(b, head // UH, head % UH, k, n)
                    elif not last:
                        scores_for_max(b + 1, 0, head - GB, k, n)

                new_maxima = g % 4 == 2 and not (last and g // 4 == 3)
                ahead(0, 2)
                if new_maxima:
                    maxima(b * HALVES + g // 4 + 1, (g // 4 + 1) % 2, b * GB + g)
                if g >= 2:
                    with_v(b, g - 2)
                elif not first:
                    with_v(b - 1, GB - 2 + g)
                ahead(2, 1)
                scores(b, g, 0, 2, new_maxima)
                ahead(3, 1)
                scores(b, g, 2, 2)
                if g == 1 and not first:
                    output_sums(b - 1, 1)
                if g == 2 and not first:
                    attn_turned()
                if g == 3 and not first:
                    project()
                if g == GROUPS + 1:
                    output_sums(b, 0)

            def experts(b):
                pe.wait_ge(s_exp, b * (4 * GB) + 4 * (GB + 4))
                for q in range(2):
                    e = b * 2 - 2 * EXPERTS_FROM + q
                    pe.wait_ge(s_xe, e * 16 + 16)
                    chunks = []
                    for (c0, w) in CH:
                        turned(lambda k: xe[:, c0 // P + k, :], w // P)
                        chunks.append(d.value())
                    pe.wait_ge(s_w[q], b * 64 - (EXPERTS_FROM - 1) * 64)
                    for hc in range(HC):
                        for c, (c0, w) in enumerate(CH):
                            k = hc * NCH + c
                            if hc == 0:
                                pe.wait_ge(s_dd, chunks[c])
                            if k >= 4:
                                pe.wait_ge(s_ge, e * (HC * NCH) + k - 3)
                            nc.tensor.matmul(bA[k % 4][:, 0:w], wfc[q][:, hc * P:(hc + 1) * P], xeT[:, c0:c0 + w], start=True,
                                             stop=True).then_inc(s_up, 1)
                    pe.wait_ge(s_ge, e * (HC * NCH) + HC * NCH)
                    for (c0, w) in CH:
                        to = free()
                        for k in range(w // P):
                            for hc in range(HC):
                                last = nc.tensor.matmul(to[:, k * P:(k + 1) * P], hid[:, hc, c0 + k * P:c0 + (k + 1) * P],
                                                        wpj[q][:, hc, :], start=(hc == 0), stop=(hc == HC - 1))
                        done(last)

            pe.wait_ge(s_ve, 2 * B)
            pe.wait_ge(s_ranks, 1)
            for s in range(LEAD):
                scores_for_max(0, 0, s, 0, TT)
                if s == 4:
                    pe.wait_ge(s_xT, B)
                    maxima(0, 0)
            pe.wait_ge(s_ne, 1)
            pe.wait_ge(s_lo, 2 * B)
            for g in range(4):
                group(0, g, first=True)

            def turn(b, with_experts, last):
                for g in range(4, GB):
                    group(b, g, last)
                if last:
                    with_v(b, GB - 2)
                    with_v(b, GB - 1)
                    output_sums(b, 1)
                    pe.wait_ge(s_dd, d.value())
                    turned(lambda k: attn[:, k, :])
                    project(0)
                    return
                for g in range(4):
                    group(b + 1, g)
                if with_experts:
                    experts(b)

            each_turn(pe, [(d, D_TURN, D_EXPERTS)], turn)


def kernel(L0_attn_x, L0_attn_wq_w, L0_attn_wq_b, L0_attn_wk_w, L0_attn_wk_b, L0_attn_wv_w, L0_attn_wv_b, L0_attn_wo_w,
           L0_attn_wo_b, L0_ffn_gate_w, L0_ffn_c_fc, L0_ffn_fc_bias, L0_ffn_c_proj, L0_ffn_proj_bias):
    import numpy as np
    import concourse.bacc as bacc
    from concourse.bass_utils import run_bass_kernel_spmd

    def turned(w):
        return np.ascontiguousarray(np.asarray(w).T)

    tail = np.zeros((5, 2, T), np.float32)
    tail[0:2, 0] = 1.0
    tail[2:4, 1] = 1.0
    tail[4] = 1.0
    keys = np.concatenate([E - np.arange(E), CAP * np.arange(E)]).astype(np.float32)
    ins = {
        "x": np.asarray(L0_attn_x).reshape(N, C),
        "wq": turned(L0_attn_wq_w), "wk": turned(L0_attn_wk_w), "wv": turned(L0_attn_wv_w),
        "gate": np.asarray(L0_ffn_gate_w), "wo": turned(L0_attn_wo_w),
        "bq": np.asarray(L0_attn_wq_b).reshape(C, 1), "bk": np.asarray(L0_attn_wk_b).reshape(C, 1),
        "bv": np.asarray(L0_attn_wv_b).reshape(1, C), "bo": np.asarray(L0_attn_wo_b).reshape(1, C),
        "c_fc": np.asarray(L0_ffn_c_fc),
        "fcb": np.ascontiguousarray(np.asarray(L0_ffn_fc_bias).reshape(E, HC, P).transpose(0, 2, 1)),
        "c_proj": np.asarray(L0_ffn_c_proj), "pjb": np.asarray(L0_ffn_proj_bias),
        "ident": np.eye(P, dtype=np.float32),
        "prefix": np.triu(np.ones((P, P), np.float32), 1),
        "keys": np.tile(keys, (P, 1)),
        "tail": tail,
    }
    nc = bacc.Bacc("TRN2", target_bir_lowering=False, num_devices=1)
    arrays, args = {}, []
    for name, a in ins.items():
        a = np.ascontiguousarray(a)
        arrays[f"in_{name}"] = a
        args.append(nc.dram_tensor(f"in_{name}", a.shape, mybir.dt.from_np(a.dtype), kind="ExternalInput").ap())
    out = nc.dram_tensor("out_0", [N, C], F32, kind="ExternalOutput").ap()
    build(nc, *args, out)
    r = run_bass_kernel_spmd(nc, [arrays], core_ids=[0])
    return r.results[0]["out_0"].reshape(B, T, C)
```

```python
from contextlib import ExitStack

import concourse.bass as bass
from concourse import mybir
from concourse.alu_op_type import AluOpType as ALU

F32 = mybir.dt.float32
F32R = mybir.dt.float32r
I32 = mybir.dt.int32
ACT = mybir.ActivationFunctionType
AX = mybir.AxisListType

P = 128
B, T, C = 8, 512, 128
H, DH = 16, 8
E, TOPK = 8, 2
HID = 4 * C
N = B * T
CAP = int(1.25 * N * TOPK / E)
SLOTS = E * CAP
NT = N // P
TT = T // P
HC = HID // P
ST = CAP // P
SCALE = float(DH) ** -0.5
EPS = 1e-5
MASKED = -float(2 ** 100)
UH = 8
UNITS = H // UH
GROUPS = 2 * TT
GB = UNITS * GROUPS
LEAD = 6
HALVES = 2 * UNITS
ROWS = 4 * DH
TAIL = 2 * ROWS
MASKROW = TAIL + 4
BIGSLOT = 4.0 * SLOTS
CH = [(0, 512), (512, 512), (1024, 256)]
NCH = len(CH)
KN = TOPK * NT
EXPERTS_FROM, EXPERTS_TO = 2, 6
assert 2 * (EXPERTS_TO - EXPERTS_FROM) == E
COMBINED_BY_POOL = 2
assert LEAD >= B - COMBINED_BY_POOL
N_CONST, N_LATER = 8, 4
WR_DMAS, LOAD_DMAS = 3, 11
ZERO_DMAS, ROW_DMAS = 10, 6
D_FIRST = (LEAD + 4) * TT
D_BANK = -D_FIRST % 3
D_TURN = GB * TT + 5
D_EXPERTS = 2 * 2 * NCH
assert D_TURN % 3 == 0 and D_EXPERTS % 3 == 0
D_EXPERTS_FROM = D_FIRST + EXPERTS_FROM * D_TURN + D_TURN


class Count:

    def __init__(self, base=0):
        self.base, self.local, self.turn, self.per, self.since = base, 0, None, 0, 0

    def enter(self, turn, per):
        self.base, self.local = self.base + self.local, 0
        self.turn, self.per = turn, per
        self.since = 0

    def leave(self, turns):
        assert self.local == self.per, (self.local, self.per)
        self.base, self.local, self.turn = self.base + turns * self.per, 0, None

    def step(self, k=1):
        self.local += k
        self.since += k

    def least(self, k=0):
        return self.base + self.local + k

    def value(self, k=0):
        if self.turn is None:
            return self.least(k)
        return self.turn * self.per + self.least(k)


BETWEEN = [("rows", 0), ("rows", 1), ("results", 0), ("rows", 2), ("results", 1), ("results", 2)]


def build(nc, x, wq, wk, wv, gate, wo, bq, bk, bv, bo, c_fc, fcb, c_proj, pjb, ident_d, prefix_d, keys_d, tail_d, out):
    with ExitStack() as ctx:
        def sb(name, shape, dt=F32):
            return ctx.enter_context(nc.sbuf_tensor(name, shape, dt))

        def ps(name):
            return ctx.enter_context(nc.psum_tensor(name, [P, 512], F32))

        def sem(name):
            return ctx.enter_context(nc.semaphore(name))

        q_parts = nc.dram_tensor("q_parts", [B, C, 2, T], F32, kind="Internal").ap()
        k_parts = nc.dram_tensor("k_parts", [B, C, 2, T], F32, kind="Internal").ap()
        mask_row = nc.dram_tensor("mask_row", [B, T], F32, kind="Internal").ap()
        slot_x = nc.dram_tensor("slot_x", [SLOTS, C], F32, kind="Internal").ap()
        slot_y = nc.dram_tensor("slot_y", [SLOTS, C], F32, kind="Internal").ap()

        ident = sb("ident", [P, P])
        prefix = sb("prefix", [P, P])
        prefix_r = sb("prefix_r", [P, P], F32R)
        ones_r = sb("ones_r", [P, P], F32R)
        ones = sb("ones", [P, P])
        keys = sb("keys", [P, 2 * E])
        wq_s, wk_s, wo_s = sb("wq_s", [C, C]), sb("wk_s", [C, C]), sb("wo_s", [C, C])
        wvg_s = sb("wvg_s", [C, C + E])
        bq_s, bk_s = sb("bq_s", [C, 1]), sb("bk_s", [C, 1])
        bv_s, bo_s = sb("bv_s", [P, C]), sb("bo_s", [P, C])
        acc = sb("acc", [P, NT, C])
        xn_all = sb("xn_all", [P, NT, C])
        v_all = sb("v_all", [P, NT, C])
        K = [sb(f"K{u}", [P, UH, T], F32R) for u in range(UNITS)]
        Q = [sb(f"Q{u}", [P, UH // 2, T], F32R) for u in range(UNITS)]
        zeros4 = sb("zeros4", [4, 2, T], F32R)
        probs = sb("probs", [P, 8, T])
        v_aug = sb("v_aug", [P, TT, H, 32])
        nmax = [sb(f"nmax{q}", [P, TT, 4]) for q in range(2)]
        nmhl = [sb(f"nmhl{q}", [P, TT, 4, 2], F32R) for q in range(2)]
        nmT = [sb(f"nmT{q}", [8, T], F32R) for q in range(2)]
        pv_s = sb("pv_s", [P, T])
        rsum = sb("rsum", [P, TT, 4, 2])
        attn = sb("attn", [P, TT, C])
        attnT = sb("attnT", [C, T])
        hid = sb("hid", [P, HC, CAP])
        xe = sb("xe", [P, ST, C])
        xeT = [sb(f"xeT_{part}", [C, CAP], F32R) for part in ("hi", "lo")]
        ye = sb("ye", [P, ST, C])
        wfc = [sb(f"wfc{q}", [C, HID]) for q in range(2)]
        wfc_parts = [[sb(f"wfc{q}_{part}", [C, HID], F32R) for part in ("hi", "lo")] for q in range(2)]
        wpj = [sb(f"wpj{q}", [P, HC, C]) for q in range(2)]
        fcb_s = [sb(f"fcb{q}", [P, HC]) for q in range(2)]
        pjb_s = [sb(f"pjb{q}", [P, C]) for q in range(2)]
        hid_f = hid[:, :, :].rearrange("p a b -> p (a b)")
        parts = {(w, q): hid_f[:, (2 * w + q) * 2 * T:(2 * w + q + 1) * 2 * T].rearrange("p (s t) -> p s t", s=2)
                 for w in range(2) for q in range(2)}
        xst = [xe[:, TT * q:TT * (q + 1), :] for q in range(2)]
        xT = [ye[:, TT * q:TT * (q + 1), :].rearrange("p n c -> p (n c)") for q in range(2)]
        tail = probs[0:5, 0:2, :]
        scan, rank = (wfc[q][:].rearrange("p (n e) -> p n e", e=E) for q in range(2))
        total = wpj[0][:].rearrange("p h c -> p (h c)").rearrange("p (n e) -> p n e", e=E)
        r_eq, r_key = (wpj[1][:, 2 * q:2 * q + 2, :].rearrange("p h c -> p (h c)").rearrange("p (n e) -> p n e", e=E)
                       for q in range(2))
        stats = [sb(f"stats{q}", [P, TT, 6]) for q in range(2)]
        mv = [sb(f"mv{q}", [P, TT, 2]) for q in range(2)]
        var = [sb(f"var{q}", [P, TT]) for q in range(2)]
        std = [sb(f"std{q}", [P, TT]) for q in range(2)]
        rstd = [sb(f"rstd{q}", [P, TT]) for q in range(2)]
        mrow = [sb(f"mrow{q}", [1, T], F32R) for q in range(2)]
        logit = sb("logit", [P, NT, E])
        top = sb("top", [P, TOPK, NT])
        kmax = sb("kmax", [P, NT])
        hot = sb("hot", [P, KN, E], F32R)
        keep = sb("keep", [P, KN])
        gap = sb("gap", [P, NT])
        prob = sb("prob", [P, KN])
        wgt = sb("wgt", [P, KN])
        slot_f = sb("slot_f", [P, KN])
        put_f = sb("put_f", [P, KN])
        put_i = sb("put_i", [P, KN], I32)
        get_i = sb("get_i", [P, KN], I32)

        bA = [ps(f"bA{n}") for n in range(4)]
        bD = [ps(f"bD{n}") for n in range(3)]
        bPV = ps("bPV")

        s_ident = sem("s_ident")
        s_const = sem("s_const")
        s_later = sem("s_later")
        s_fill = sem("s_fill")
        s_rows = sem("s_rows")
        s_xin = [sem("s_xin0"), sem("s_xin1")]
        s_var = sem("s_var")
        s_std = sem("s_std")
        s_xn = sem("s_xn")
        s_tp = sem("s_tp")
        s_copy = sem("s_copy")
        s_bo = sem("s_bo")
        s_xT = sem("s_xT")
        s_qk = sem("s_qk")
        s_hi = sem("s_hi")
        s_lo = sem("s_lo")
        s_vg = sem("s_vg")
        s_ve = sem("s_ve")
        s_mask = sem("s_mask")
        s_wr = [sem("s_wr0"), sem("s_wr1")]
        s_prefix = sem("s_prefix")
        s_hot = sem("s_hot")
        s_rank = sem("s_rank")
        s_gap = sem("s_gap")
        s_gexp = sem("s_gexp")
        s_ranks = sem("s_ranks")
        s_scan = sem("s_scan")
        s_prob = sem("s_prob")
        s_slots = sem("s_slots")
        s_put = sem("s_put")
        s_chain = sem("s_chain")
        s_load = [[sem(f"s_load{u}{q}") for q in range(2)] for u in range(UNITS)]
        s_st = sem("s_st")
        s_exp = sem("s_exp")
        s_pv = sem("s_pv")
        s_pvo = sem("s_pvo")
        s_d = sem("s_d")
        s_dd = sem("s_dd")
        s_nm = sem("s_nm")
        s_nt = sem("s_nt")
        s_ne = sem("s_ne")
        s_nq = [sem("s_nq0"), sem("s_nq1")]
        s_vaug = sem("s_vaug")
        s_w = [sem("s_w0"), sem("s_w1")]
        s_xe = sem("s_xe")
        s_xhi = sem("s_xhi")
        s_split = sem("s_split")
        s_up = sem("s_up")
        s_ge = sem("s_ge")
        s_zero = sem("s_zero")
        s_slot = sem("s_slot")
        s_get = [sem(f"s_get{b}") for b in range(B)]
        s_comb_p = sem("s_comb_p")
        s_comb = sem("s_comb")
        s_out = sem("s_out")

        x_v = x.rearrange("(n p) c -> p n c", p=P)
        out_v = out.rearrange("(n p) c -> p n c", p=P)
        slot_x_v = slot_x.rearrange("(e s p) c -> e p s c", s=ST, p=P)
        slot_y_v = slot_y.rearrange("(e s p) c -> e p s c", s=ST, p=P)

        def rows(t, b, k=0, n=TT):
            return t[:, bass.ds(b * TT + k, n), :]

        def wait(eng, s, value):
            if not isinstance(value, int) or value > 0:
                eng.wait_ge(s, value)

        def heads(new_maxima):
            return (1, 2, 3, 0) if new_maxima else (0, 1, 2, 3)

        def each_batch(eng, step):
            for q in range(2):
                step(q, q)
            with eng.Fori(1, B // 2) as i:
                for q in range(2):
                    step(i * 2 + q, q)

        def each_turn(eng, counts, turn):
            for start, end, experts in ((0, EXPERTS_FROM, False), (EXPERTS_FROM, EXPERTS_TO, True)):
                with eng.Fori(start, end) as b:
                    for c, per, more in counts:
                        c.enter(b - start if start else b, per + more * experts)
                    turn(b, experts, False)
                for c, _, _ in counts:
                    c.leave(end - start)
            for b in range(EXPERTS_TO, B):
                for c, _, _ in counts:
                    c.since = 0
                turn(b, False, b == B - 1)

        def gathered(b, n):
            n += (b % 4) * TOPK * TT
            return xn_all[:, n, :] if b < 4 else hid_f[:, n * C:(n + 1) * C]

        block = ctx.enter_context(nc.Block())

        @block.sync
        def _(sp):
            def load_x(b, q):
                sp.dma_start(rows(acc, b), rows(x_v, b)).then_inc(s_xin[q], 16)

            load_x(0, 0)
            sp.dma_start(ident[:], ident_d).then_inc(s_ident, 16)
            load_x(1, 1)
            for t, src in ((wq_s, wq), (bq_s, bq), (wk_s, wk), (bk_s, bk)):
                sp.dma_start(t[:], src).then_inc(s_const, 16)
            sp.dma_start(wvg_s[:, 0:C], wv).then_inc(s_const, 16)
            sp.dma_start(wvg_s[:, C:C + E], gate).then_inc(s_const, 16)
            sp.dma_start(bv_s[:], bv.to_broadcast([P, C])).then_inc(s_const, 16)
            sp.dma_start(bo_s[:], bo.to_broadcast([P, C])).then_inc(s_const, 16)
            sp.dma_start(tail, tail_d).then_inc(s_later, 16)
            for t, src in ((prefix, prefix_d), (keys, keys_d), (wo_s, wo)):
                sp.dma_start(t[:], src).then_inc(s_later, 16)

            def write_stacks(b, q):
                sp.wait_ge(s_lo, b * 2 + 2)
                sp.dma_start(q_parts[b], parts[0, q]).then_inc(s_wr[q], 16)
                sp.dma_start(k_parts[b], parts[1, q]).then_inc(s_wr[q], 16)
                sp.wait_ge(s_mask, b + 1)
                sp.dma_start(mask_row[bass.ds(b, 1), :], mrow[q][:].bitcast(F32)).then_inc(s_wr[q], 16)

            def step(b, q):
                sp.wait_ge(s_xn, b + 1)
                load_x(b + 2, q)
                if not isinstance(b, int) or b > 0:
                    write_stacks(b - 1, 1 - q)

            step(0, 0)
            with sp.Fori(0, B // 2 - 2) as i:
                for q in range(2):
                    step(i * 2 + q + 1, 1 - q)
            step(B - 3, 1)
            write_stacks(B - 3, 1)

            def load_quad(b, u, q):
                pair0 = u * (UH // 2) + 2 * q
                qs = q_parts[b].rearrange("(pair c) s t -> (c s) pair t", c=2 * DH)
                ks = k_parts[b].rearrange("(pair e c) s t -> e (c s) pair t", e=2, c=DH)
                qp = q_parts[b].rearrange("(pair c) s t -> s c pair t", c=2 * DH)
                kp = k_parts[b].rearrange("(pair e c) s t -> s e c pair t", e=2, c=DH)
                qd = Q[u][:, 2 * q:2 * q + 2, :].bitcast(F32)
                kd = K[u][:, 4 * q:4 * q + 4, :].bitcast(F32).rearrange("p (pair e) t -> p e pair t", e=2)
                sp.dma_start(qd[0:ROWS], qs[:, pair0:pair0 + 2, :]).then_inc(s_load[u][q], 16)
                for e in range(2):
                    sp.dma_start(kd[e * 2 * DH:(e + 1) * 2 * DH, e, :, :], ks[e, :, pair0:pair0 + 2, :]
                                 ).then_inc(s_load[u][q], 16)
                for s in range(2):
                    at = ROWS + s * 2 * DH
                    sp.dma_start(qd[at:at + 2 * DH], qp[s, :, pair0:pair0 + 2, :]).then_inc(s_load[u][q], 16)
                    for e in range(2):
                        sp.dma_start(kd[at + e * DH:at + (e + 1) * DH, e, :, :], kp[1 - s, e, :, pair0:pair0 + 2, :]
                                     ).then_inc(s_load[u][q], 16)
                sp.dma_start(K[u][MASKROW:MASKROW + 1, 4 * q:4 * q + 4, :].bitcast(F32),
                             mask_row[bass.ds(b, 1), None, :].to_broadcast([1, 4, T])).then_inc(s_load[u][q], 16)
                sp.dma_start(Q[u][TAIL:TAIL + 4, 2 * q:2 * q + 2, :].bitcast(F32), zeros4[:].bitcast(F32)).then_inc(s_load[u][q], 16)

            def max_rows(u, q, m):
                sp.wait_ge(s_ne, m + 1)
                for pair in range(2):
                    sp.dma_start(Q[u][TAIL:TAIL + 4, 2 * q + pair, :].bitcast(F32),
                                 nmT[q][4 * pair:4 * pair + 4, :].bitcast(F32)).then_inc(s_nq[q], 16)

            sp.wait_ge(s_rows, ROW_DMAS * 16)
            sp.wait_ge(s_wr[0], (B // 2 - 1) * WR_DMAS * 16)
            for q in range(2):
                load_quad(0, 0, q)
            write_stacks(B - 2, 0)
            write_stacks(B - 1, 1)
            for q in range(2):
                load_quad(0, 1, q)
                max_rows(0, q, q)
            for q in range(2):
                sp.wait_ge(s_wr[q], B // 2 * WR_DMAS * 16)

            def load_rows(e):
                sp.dma_start(xe[:], slot_x_v[e]).then_inc(s_xe, 16)

            def load_experts(b):
                e = b * 2 - 2 * EXPERTS_FROM
                sp.wait_ge(s_put, KN * 16)
                load_rows(e)
                for q in range(2):
                    sp.dma_start(wfc[q][:], c_fc[e + q]).then_inc(s_w[q], 16)
                    sp.dma_start(wpj[q][:], c_pj_v[e + q]).then_inc(s_w[q], 16)
                    sp.dma_start(fcb_s[q][:], fcb[e + q]).then_inc(s_w[q], 16)
                    sp.dma_start(pjb_s[q][:], pjb[e + q].to_broadcast([P, C])).then_inc(s_w[q], 16)

            def experts(b):
                e0 = b * 2 - 2 * EXPERTS_FROM
                before = (b - EXPERTS_FROM) * (D_TURN + D_EXPERTS) + D_EXPERTS_FROM
                sp.wait_ge(s_dd, before + NCH)
                load_rows(e0 + 1)
                for q in range(2):
                    sp.wait_ge(s_dd, before + (3 + q) * NCH)
                    sp.dma_start(slot_y_v[e0 + q], ye[:]).then_inc(s_slot, 16)

            c_pj_v = c_proj.rearrange("e (h p) c -> e p h c", p=P)

            def turn(b, with_experts, last):
                through = b * (4 * GB)
                m = b * HALVES + 2
                max_rows(1, 0, m)
                if last:
                    max_rows(1, 1, m + 1)
                    return
                sp.wait_ge(s_st, through + 4 * 4)
                load_quad(b + 1, 0, 0)
                sp.wait_ge(s_st, through + 4 * 8)
                load_quad(b + 1, 0, 1)
                max_rows(1, 1, m + 1)
                sp.wait_ge(s_st, through + 4 * 12)
                load_quad(b + 1, 1, 0)
                max_rows(0, 0, m + 2)
                if with_experts:
                    load_experts(b)
                sp.wait_ge(s_st, through + 4 * 16)
                load_quad(b + 1, 1, 1)
                max_rows(0, 1, m + 3)
                if with_experts:
                    experts(b)

            each_turn(sp, [], turn)
            for b in (*range(COMBINED_BY_POOL, B - 1), *range(COMBINED_BY_POOL), B - 1):
                if b < COMBINED_BY_POOL:
                    sp.wait_ge(s_comb_p, b + 1)
                else:
                    sp.wait_ge(s_comb, b + 1 - COMBINED_BY_POOL)
                sp.dma_start(rows(out_v, b), rows(acc, b)).then_inc(s_out, 16)
            sp.wait_ge(s_out, B * 16)

        @block.gpsimd
        def _(pool):
            for t in (K[0], K[1], Q[0], Q[1], zeros4):
                nc.gpsimd.memset(t[:].bitcast(F32), 0.0).then_inc(s_fill, 1)
            pool.wait_ge(s_fill, 5)
            pool.wait_ge(s_const, N_CONST * 16)
            pool.wait_ge(s_later, N_LATER * 16)
            nc.gpsimd.memset(ones_r[:].bitcast(F32), 1.0)
            nc.gpsimd.tensor_copy(prefix_r[:], prefix[:]).then_inc(s_prefix, 1)
            for u in range(UNITS):
                kt = K[u][TAIL:TAIL + 4, :, :].bitcast(F32).rearrange("p (pair e) t -> p e pair t", e=2)
                for e in range(2):
                    pool.dma_start(kt[:, e], tail[0:4, e:e + 1, :].to_broadcast([4, UH // 2, T])).then_inc(s_rows, 16)
                pool.dma_start(Q[u][MASKROW:MASKROW + 1, :, :].bitcast(F32),
                               tail[4:5, 0:1, :].to_broadcast([1, UH // 2, T])).then_inc(s_rows, 16)

            def front(b, q):
                pool.wait_ge(s_xn, b + 1)
                pool.wait_ge(s_xT, b + 1)
                wait(pool, s_wr[q], (b - q) * (WR_DMAS * 16 // 2))
                if not isinstance(b, int) or b > 0:
                    add_bv(b - 1)
                nc.gpsimd.tensor_scalar(mrow[q][:], xT[q][0:1, :], 0.0, MASKED, ALU.is_equal, ALU.mult).then_inc(s_mask, 1)

            def add_bv(b):
                pool.wait_ge(s_ve, b * 2 + 2)
                nc.gpsimd.tensor_tensor(rows(v_all, b), rows(v_all, b), bv_s[:, None, :].to_broadcast([P, TT, C]), ALU.add)

            each_batch(pool, front)
            add_bv(B - 1)
            nc.gpsimd.memset(v_aug[:], 0.0).then_inc(s_fill, 1)
            pool.wait_ge(s_fill, 6)
            for q in range(2):
                va = v_aug[:].rearrange("p j (u r) c -> p (j u) r c", u=UNITS)
                nc.gpsimd.memset(va[:, :, 4 * q:4 * q + 4, 16 + q], 1.0).then_inc(s_fill, 1)

            steps = [0]

            def link(ins):
                ins.then_inc(s_slots, 1)
                steps[0] += 1
                pool.wait_ge(s_slots, steps[0])

            pool.wait_ge(s_ranks, 1)
            pool.wait_ge(s_scan, 1)
            flat = [t.rearrange("p n e -> p (n e)") for t in (scan[:], total[:], rank[:], hot[:].bitcast(F32))]
            link(nc.gpsimd.tensor_tensor(flat[0], flat[0], flat[1], ALU.subtract))
            link(nc.gpsimd.tensor_tensor(flat[2], flat[0], flat[2], ALU.add))
            nc.gpsimd.tensor_tensor(scan[:], hot[:].bitcast(F32), keys[:, None, E:2 * E].to_broadcast([P, KN, E]), ALU.mult)
            link(nc.gpsimd.tensor_tensor(flat[2], flat[2], flat[3], ALU.mult))
            for half in (4, 2, 1):
                nc.gpsimd.tensor_tensor(rank[:, :, 0:half], rank[:, :, 0:half], rank[:, :, half:2 * half], ALU.add)
                link(nc.gpsimd.tensor_tensor(scan[:, :, 0:half], scan[:, :, 0:half], scan[:, :, half:2 * half], ALU.add))
            r_at, r_base = rank[:, :, 0], scan[:, :, 0]
            link(nc.gpsimd.tensor_scalar(keep[:], r_at, float(CAP), None, ALU.is_lt))
            link(nc.gpsimd.tensor_tensor(slot_f[:], r_at, keep[:], ALU.mult))
            link(nc.gpsimd.tensor_tensor(slot_f[:], slot_f[:], r_base, ALU.add))
            nc.gpsimd.tensor_copy(get_i[:], slot_f[:])
            link(nc.gpsimd.tensor_scalar(put_f[:], keep[:], -BIGSLOT, BIGSLOT, ALU.mult, ALU.add))
            link(nc.gpsimd.tensor_tensor(put_f[:], put_f[:], slot_f[:], ALU.add))
            pool.wait_ge(s_prob, 1)
            nc.gpsimd.tensor_tensor(wgt[:], prob[:], keep[:], ALU.mult)
            link(nc.gpsimd.tensor_copy(put_i[:], put_f[:]))

            for q in range(2):
                pool.wait_ge(s_wr[q], B // 2 * WR_DMAS * 16)
            per = SLOTS * C // P // ZERO_DMAS
            nc.gpsimd.memset(hid_f[:, 0:per], 0.0).then_inc(s_fill, 1)
            pool.wait_ge(s_fill, 9)
            pool.wait_ge(s_nq[0], 32)
            for h in range(ZERO_DMAS):
                pool.dma_start(slot_x.rearrange("(p h r) c -> h p (r c)", p=P, h=ZERO_DMAS)[h], hid_f[:, 0:per]
                               ).then_inc(s_zero, 16)
                pool.wait_ge(s_zero, h * 16 + 16)
            nc.gpsimd.tensor_tensor(acc[:], acc[:], bo_s[:, None, :].to_broadcast([P, NT, C]), ALU.add).then_inc(s_bo, 1)
            pool.wait_ge(s_copy, B)
            for k in range(TOPK):
                for n in range(NT):
                    col = k * NT + n
                    pool.indirect_dma_start(slot_x, bass.IndirectOffsetOnAxis(ap=put_i[:, col:col + 1], axis=0),
                                            xn_all[:, n, :], None, bounds_check=SLOTS - 1, oob_is_err=False
                                            ).then_inc(s_put, 16)
            with pool.Fori(EXPERTS_FROM, EXPERTS_TO) as b:
                for q in range(2):
                    steps_before = (b * 2 - 2 * EXPERTS_FROM + q) * 2
                    pool.wait_ge(s_w[q], b * 64 - (EXPERTS_FROM - 1) * 64)
                    wide = "p (h c) -> p h c"
                    nc.gpsimd.tensor_tensor(wfc_parts[q][0][:].rearrange(wide, c=P), wfc[q][:].rearrange(wide, c=P),
                                            ones[:, None, :].to_broadcast([P, HC, P]), ALU.mult).then_inc(s_split, 1)
                    pool.wait_ge(s_split, steps_before + 1)
                    nc.gpsimd.tensor_tensor(wfc_parts[q][1][:], wfc[q][:], wfc_parts[q][0][:].bitcast(F32), ALU.subtract
                                            ).then_inc(s_split, 1)
            pool.wait_ge(s_slot, E * 16 + 16)
            for b in range(B):
                for k in range(TOPK):
                    for n in range(TT):
                        col = k * NT + b * TT + n
                        pool.indirect_dma_start(gathered(b, k * TT + n), None, slot_y,
                                                bass.IndirectOffsetOnAxis(ap=get_i[:, col:col + 1], axis=0),
                                                bounds_check=SLOTS - 1, oob_is_err=False).then_inc(s_get[b], 16)
            for b in range(B):
                pool.wait_ge(s_get[b], TOPK * TT * 16)
            for b in range(COMBINED_BY_POOL):
                got = xn_all[:, b * TOPK * TT:(b + 1) * TOPK * TT, :].rearrange("p (k n) c -> p k n c", k=TOPK)
                weights = wgt[:].rearrange("p (k n) -> p k n", k=TOPK)[:, :, b * TT:(b + 1) * TT]
                for k in range(TOPK):
                    last = nc.gpsimd.tensor_tensor(got[:, k], got[:, k],
                                                   weights[:, k, :, None].to_broadcast([P, TT, C]), ALU.mult)
                link(last)
                link(nc.gpsimd.tensor_tensor(rows(acc, b), rows(acc, b), got[:, 0], ALU.add))
                nc.gpsimd.tensor_tensor(rows(acc, b), rows(acc, b), got[:, 1], ALU.add).then_inc(s_comb_p, 1)

        @block.scalar
        def _(act):
            def high(b, q):
                wait(act, s_wr[q], (b - q) * (WR_DMAS * 16 // 2))
                for w, bias in ((0, bq_s), (1, bk_s)):
                    act.wait_ge(s_qk, b * 2 + w + 1)
                    nc.scalar.activation(parts[w, q][:, 0, :].bitcast(F32R), bA[2 + w][:], ACT.Identity, bias=bias[:]
                                         ).then_inc(s_hi, 1)

            def values(b):
                for h in range(2):
                    act.wait_ge(s_vg, b * 2 + h + 1)
                    pv = bD[h][:, 0:2 * (C + E)].rearrange("p (n c) -> p n c", n=2)
                    nc.scalar.copy(rows(v_all, b, 2 * h, 2), pv[:, :, 0:C])
                    nc.scalar.copy(rows(logit, b, 2 * h, 2), pv[:, :, C:C + E]).then_inc(s_ve, 1)

            def front(b, q):
                act.wait_ge(s_var, b + 1)
                nc.scalar.activation(std[q][:], var[q][:], ACT.Sqrt).then_inc(s_std, 1)
                if not isinstance(b, int) or b > 0:
                    high(b - 1, 1 - q)
                    values(b - 1)
                act.wait_ge(s_tp, b + 1)
                wait(act, s_vg, (b - 1) * 2)
                wait(act, s_mask, b - 1)
                nc.scalar.copy(xT[q], bA[q][:]).then_inc(s_xT, 1)
                nc.scalar.copy(rows(xn_all, b), xst[q]).then_inc(s_copy, 1)

            each_batch(act, front)
            high(B - 1, 1)
            values(B - 1)
            act.wait_ge(s_gap, 1)
            nc.scalar.activation(gap[:], gap[:], ACT.Exp).then_inc(s_gexp, 1)
            act.wait_ge(s_rank, 1)
            nc.scalar.copy(rank[:].rearrange("p n e -> p (n e)"), bA[1][:])
            nc.scalar.copy(total[:].rearrange("p n e -> p (n e)"), bPV[:]).then_inc(s_ranks, 1)

            def maxima(m, q, k):
                act.wait_ge(s_nt, m + 1)
                wait(act, s_nq[q], k * 32)
                nc.scalar.copy(nmT[q][:], bA[0][0:8, :]).then_inc(s_ne, 1)

            def group(b, g, last=False, first=False):
                n = b * GB + g
                new_maxima = g % 4 == 2 and not (last and g // 4 == 3)
                if new_maxima:
                    maxima(b * HALVES + g // 4 + 1, (g // 4 + 1) % 2, b * 2 + (g // 4 + 1) // 2)
                if g == 1 and not first:
                    sums(b * UNITS - 1)
                if g == GROUPS + 1:
                    sums(b * UNITS)
                if g == 1:
                    fill_v(b)
                for i, h in enumerate(heads(new_maxima)):
                    act.wait_ge(s_st, n * 4 + i + 1)
                    if i == 0:
                        wait(act, s_pv, n - 1)
                    nc.scalar.activation(probs[:, (g % 2) * 4 + h, :], bA[h][:], ACT.Exp, scale=SCALE).then_inc(s_exp, 1)

            def fill_v(b):
                wait(act, s_pv, b * GB)
                if isinstance(b, int) and b == 0:
                    act.wait_ge(s_fill, 8)
                va = v_aug[:].rearrange("p j (u r) c -> p (j u) r c", u=UNITS)
                vs = rows(v_all, b).rearrange("p j (u r c) -> p (j u) r c", u=UNITS, c=DH)
                for q in range(2):
                    last = nc.scalar.copy(va[:, :, 4 * q:4 * q + 4, DH * q:DH * (q + 1)], vs[:, :, 4 * q:4 * q + 4, :])
                last.then_inc(s_vaug, 1)

            def sums(unit):
                act.wait_ge(s_pv, (unit + 1) * GROUPS)
                nc.scalar.copy(pv_s[:], bPV[:]).then_inc(s_pvo, 1)

            def experts(b):
                before = (b - EXPERTS_FROM) * (D_TURN + D_EXPERTS) + D_EXPERTS_FROM
                for q in range(2):
                    e = b * 2 - 2 * EXPERTS_FROM + q
                    for c, (c0, w) in enumerate(CH):
                        at = NCH + BETWEEN.index(("rows", c)) if q else c
                        act.wait_ge(s_d, before + at + 1)
                        nc.scalar.copy(xeT[0][:, c0:c0 + w], bD[at % 3][:, 0:w]).then_inc(s_xhi, 1)
                    for hc in range(HC):
                        for c, (c0, w) in enumerate(CH):
                            k = hc * NCH + c
                            act.wait_ge(s_up, e * (HC * NCH) + k + 1)
                            nc.scalar.activation(hid[:, hc, c0:c0 + w], bA[k % 4][:, 0:w], ACT.Gelu,
                                                 bias=fcb_s[q][:, hc:hc + 1]).then_inc(s_ge, 1)

            maxima(0, 0, 0)
            for g in range(4):
                group(0, g, first=True)

            def turn(b, with_experts, last):
                for g in range(4, GB):
                    group(b, g, last)
                if last:
                    sums(b * UNITS + 1)
                    return
                for g in range(4):
                    group(b + 1, g)
                if with_experts:
                    experts(b)

            each_turn(act, [], turn)

        @block.vector
        def _(dve):
            chain = [0]

            def link(ins):
                ins.then_inc(s_chain, 1)
                chain[0] += 1
                dve.wait_ge(s_chain, chain[0])

            F = 3

            def norm(b, q):
                dve.wait_ge(s_xin[q], (b - q) * 8 + 16)
                for k in range(TT):
                    last = nc.vector.bn_stats(stats[q][:, k, :], rows(acc, b, k, 1).rearrange("p n c -> p (n c)"))
                last.then_inc(s_chain, 1)
                dve.wait_ge(s_chain, b * F + 1)
                nc.vector.memset(var[q][:], 0.0)
                for k in range(TT):
                    last = nc.vector.bn_aggr(mv[q][:, k, :], stats[q][:, k, :])
                last.then_inc(s_chain, 1)
                dve.wait_ge(s_chain, b * F + 2)
                nc.vector.tensor_scalar(var[q][:], mv[q][:, :, 1], EPS, None, ALU.add).then_inc(s_var, 1)
                dve.wait_ge(s_std, b + 1)
                nc.vector.reciprocal(rstd[q][:], std[q][:]).then_inc(s_chain, 1)
                dve.wait_ge(s_chain, b * F + 3)
                wait(dve, s_tp, b - 1)
                wait(dve, s_copy, b - 1)
                for k in range(TT):
                    last = nc.vector.tensor_scalar(xst[q][:, k, :], rows(acc, b, k, 1).rearrange("p n c -> p (n c)"),
                                                   mv[q][:, k, 0:1], rstd[q][:, k:k + 1], ALU.subtract, ALU.mult)
                last.then_inc(s_xn, 1)

            def late(b, q):
                for w, bias in ((0, bq_s), (1, bk_s)):
                    dve.wait_ge(s_hi, b * 2 + w + 1)
                    nc.vector.scalar_tensor_tensor(out=parts[w, q][:, 1, :].bitcast(F32R), in0=bA[2 + w][:], scalar=bias[:],
                                                   in1=parts[w, q][:, 0, :], op0=ALU.add, op1=ALU.subtract).then_inc(s_lo, 1)
            def front(b, q):
                norm(b, q)
                if not isinstance(b, int) or b > 0:
                    late(b - 1, 1 - q)

            nc.vector.memset(ones[:], 1.0).then_inc(s_slot, 16)
            each_batch(dve, front)
            late(B - 1, 1)
            chain[0] = B * F
            dve.wait_ge(s_later, N_LATER * 16)

            lg = logit[:]
            hot_k = hot[:].rearrange("p (k n) e -> p k n e", k=TOPK)
            wide = [P, NT, E]
            dve.wait_ge(s_ve, 2 * B)
            for k in range(TOPK):
                link(nc.vector.tensor_reduce(top[:, k, :], lg, AX.X, ALU.max))
                link(nc.vector.tensor_tensor(r_eq[:], lg, top[:, k, :, None].to_broadcast(wide), ALU.is_equal))
                link(nc.vector.tensor_tensor(r_key[:], r_eq[:], keys[:, None, 0:E].to_broadcast(wide), ALU.mult))
                link(nc.vector.tensor_reduce(kmax[:], r_key[:], AX.X, ALU.max))
                ins = nc.vector.tensor_tensor(hot_k[:, k], r_key[:], kmax[:, :, None].to_broadcast(wide), ALU.is_equal)
                if k == TOPK - 1:
                    ins.then_inc(s_hot, 1)
                else:
                    link(ins)
                    link(nc.vector.scalar_tensor_tensor(out=lg, in0=hot_k[:, k].bitcast(F32), scalar=MASKED, in1=lg, op0=ALU.mult,
                                                        op1=ALU.add))
            nc.vector.tensor_tensor(gap[:], top[:, 1, :], top[:, 0, :], ALU.subtract).then_inc(s_gap, 1)
            d = Count()
            d.since = D_BANK
            own = Count()
            own.step(chain[0])

            def chained(ins):
                ins.then_inc(s_chain, 1)
                own.step()
                dve.wait_ge(s_chain, own.value())

            def bank():
                return bD[d.since % 3]

            def take():
                dve.wait_ge(s_d, d.value(1))

            def scores_max(s):
                q, head = (s // 4) % 2, s % 4
                for k in range(TT):
                    take()
                    nc.vector.tensor_reduce(nmax[q][:, k, head:head + 1], bank()[:], AX.X, ALU.max, negate=True
                                            ).then_inc(s_dd, 1)
                    d.step()
                if head == 3:
                    dve.wait_ge(s_dd, d.value())
                    chained(nc.vector.tensor_copy(nmhl[q][:, :, :, 0], nmax[q][:]))
                    nc.vector.tensor_tensor(nmhl[q][:, :, :, 1], nmax[q][:], nmhl[q][:, :, :, 0].bitcast(F32), ALU.subtract
                                            ).then_inc(s_nm, 1)

            def normalise(u):
                take()
                src = bank()[:].rearrange("p (k c) -> p k c", c=P)
                sums = bank()[:].rearrange("p (kg c) -> p kg c", c=32)[:, :, 2 * DH:2 * DH + 2]
                chained(nc.vector.reciprocal(rsum[:].rearrange("p k g q -> p (k g) q"), sums))
                for q in range(2):
                    o = attn[:, :, u * 64 + q * 32:u * 64 + (q + 1) * 32].rearrange("p k (g c) -> p k g c", c=DH)
                    i0 = src.rearrange("p k (g c) -> p k g c", c=32)[:, :, :, DH * q:DH * (q + 1)]
                    last = nc.vector.tensor_tensor(o, i0, rsum[:, :, :, q:q + 1].to_broadcast([P, TT, 4, DH]), ALU.mult)
                last.then_inc(s_dd, 1)
                d.step()

            def take_attnT():
                take()
                nc.vector.tensor_copy(attnT[:], bank()[:]).then_inc(s_dd, 1)
                d.step()

            def take_out(b, done=s_dd):
                dve.wait_ge(s_bo, 1)
                for half in range(2):
                    take()
                    to = rows(acc, b, half * (TT // 2), TT // 2)
                    ins = nc.vector.tensor_tensor(to, bank()[:, 0:TT // 2 * C].rearrange("p (k c) -> p k c", c=C), to, ALU.add)
                    ins.then_inc(s_dd if half == 0 else done, 1)
                    d.step()

            def experts(b):
                def rows_in(e, c):
                    c0, w = CH[c]
                    dve.wait_ge(s_xhi, e * NCH + c + 1)
                    nc.vector.tensor_tensor(xeT[1][:, c0:c0 + w], bank()[:, 0:w], xeT[0][:, c0:c0 + w].bitcast(F32),
                                        ALU.subtract).then_inc(s_dd, 1)
                    d.step()

                def results(e, q, c):
                    if c == 0:
                        dve.wait_ge(s_slot, e * 16 + 16)
                    take()
                    c0, w = CH[c]
                    k0, nk = c0 // P, w // P
                    nc.vector.tensor_tensor(ye[:, k0:k0 + nk, :], bank()[:, 0:w].rearrange("p (k c) -> p k c", c=C),
                                            pjb_s[q][:, None, :].to_broadcast([P, nk, C]), ALU.add).then_inc(s_dd, 1)
                    d.step()

                e0 = b * 2 - 2 * EXPERTS_FROM
                for c in range(NCH):
                    rows_in(e0, c)
                for kind, c in BETWEEN:
                    if kind == "rows":
                        rows_in(e0 + 1, c)
                    else:
                        results(e0, 0, c)
                for c in range(NCH):
                    results(e0 + 1, 1, c)

            def combine(b):
                dve.wait_ge(s_get[b], TOPK * TT * 16)
                for k in range(TOPK):
                    for n in range(TT):
                        t, col = b * TT + n, k * NT + b * TT + n
                        last = nc.vector.scalar_tensor_tensor(out=acc[:, t, :], in0=gathered(b, k * TT + n),
                                                              scalar=wgt[:, col:col + 1], in1=acc[:, t, :], op0=ALU.mult,
                                                              op1=ALU.add)
                    if k == 0 or b == B - 1:
                        chained(last)
                if b == B - 1:
                    return
                last.then_inc(s_comb, 1)

            def group(b, g, last=False, first=False):
                if not last or g + LEAD < GB:
                    scores_max((g + LEAD) % UH)
                if g == 1 and not first:
                    normalise(1)
                if g == 2 and not first:
                    take_attnT()
                if g == 3 and not first:
                    take_out(b - 1)
                if g == GROUPS + 1:
                    normalise(0)

            scores_max(0)
            dve.wait_ge(s_gexp, 1)
            chained(nc.vector.tensor_scalar(kmax[:], gap[:], 1.0, None, ALU.add))
            chained(nc.vector.reciprocal(prob[:, 0:NT], kmax[:]))
            nc.vector.tensor_tensor(prob[:, NT:KN], prob[:, 0:NT], gap[:], ALU.mult).then_inc(s_prob, 1)
            dve.wait_ge(s_ranks, 1)
            for e in range(E):
                last = nc.vector.tensor_tensor_scan(scan[:, :, e], ones[:, 0:KN], total[:, :, e], 0.0, ALU.mult, ALU.add)
            last.then_inc(s_scan, 1)

            for s in range(1, LEAD):
                scores_max(s)
            for g in range(4):
                group(0, g, first=True)

            def turn(b, with_experts, last):
                for g in range(4, GB):
                    group(b, g, last)
                    if last and g + LEAD >= GB and g + LEAD - GB < B - COMBINED_BY_POOL:
                        combine(g + LEAD - GB + COMBINED_BY_POOL)
                if last:
                    normalise(1)
                    take_attnT()
                    take_out(b, s_comb)
                    return
                for g in range(4):
                    group(b + 1, g)
                if with_experts:
                    experts(b)

            each_turn(dve, [(d, D_TURN, D_EXPERTS), (own, HALVES + UNITS, 0)], turn)
        @block.tensor
        def _(pe):
            def products(b, q):
                pe.wait_ge(s_xT, b + 1)
                pe.wait_ge(s_const, N_CONST * 16)
                for w, weights in ((0, wq_s), (1, wk_s)):
                    wait(pe, s_lo, b * 2 - 1 + w)
                    nc.tensor.matmul(bA[2 + w][:], weights[:], xT[q], start=True, stop=True).then_inc(s_qk, 1)
                for h in range(2):
                    wait(pe, s_ve, b * 2 - 1 + h)
                    for n in range(2):
                        k = 2 * h + n
                        last = nc.tensor.matmul(bD[h][:, n * (C + E):(n + 1) * (C + E)], xT[q][:, k * P:(k + 1) * P], wvg_s[:],
                                                start=True, stop=True)
                    last.then_inc(s_vg, 1)

            def front(b, q):
                if not isinstance(b, int) or b > 0:
                    products(b - 1, 1 - q)
                pe.wait_ge(s_xn, b + 1)
                wait(pe, s_xT, b - 1)
                for k in range(TT):
                    last = nc.tensor.transpose(bA[q][:, k * P:(k + 1) * P], xst[q][:, k, :], ident[:])
                last.then_inc(s_tp, 1)

            pe.wait_ge(s_ident, 16)
            each_batch(pe, front)
            products(B - 1, 1)

            d = Count()
            d.since = D_BANK

            def free():
                if d.turn is not None or d.least() > 2:
                    pe.wait_ge(s_dd, d.value(-2))
                return bD[d.since % 3]

            def done(ins):
                ins.then_inc(s_d, 1)
                d.step()

            def scores_for_max(b, u, s, first, n):
                q = s // 4
                if s % 4 == 0 and first == 0:
                    pe.wait_ge(s_load[u][q], b * (LOAD_DMAS * 16) + LOAD_DMAS * 16)
                for k in range(first, first + n):
                    done(nc.tensor.matmul(free()[:], Q[u][:, s // 2, k * P:(k + 1) * P], K[u][:, s, :], start=True, stop=True))

            def maxima(m, q, n=None):
                pe.wait_ge(s_nm, m + 1)
                if n is not None:
                    pe.wait_ge(s_exp, n * 4 - 3)
                for k in range(TT):
                    last = nc.tensor.transpose(bA[0][0:8, k * P:(k + 1) * P],
                                               nmhl[q][:, k, :, :].rearrange("p h s -> p (h s)").bitcast(F32), ident[:])
                last.then_inc(s_nt, 1)

            def scores(b, g, first, n, new_maxima, last):
                u, q, j = g // GROUPS, (g % GROUPS) // 4, g % 4
                if j == 0 and first == 0:
                    pe.wait_ge(s_nq[q], (b * UNITS + u) * 32 + 32)
                for i in range(first, first + n):
                    h = heads(new_maxima)[i]
                    if h == 0 and new_maxima:
                        pe.wait_ge(s_ne, b * HALVES + g // 4 + 2)
                    else:
                        i = heads(g % 4 == 3 and not (last and g // 4 == 3)).index(h)
                        wait(pe, s_exp, (b * GB + g) * 4 - 3 + i)
                    nc.tensor.matmul(bA[h][:], K[u][:, 4 * q + h, j * P:(j + 1) * P], Q[u][:, 2 * q + h // 2, :],
                                     start=True, stop=True).then_inc(s_st, 1)

            def with_v(b, g):
                n = b * GB + g
                u, q, j = g // GROUPS, (g % GROUPS) // 4, g % 4
                pe.wait_ge(s_exp, n * 4 + 4)
                if g == 0:
                    pe.wait_ge(s_vaug, b + 1)
                if g % GROUPS == 0:
                    wait(pe, s_pvo, b * UNITS + u)
                for h in range(4):
                    last = nc.tensor.matmul(bPV[32 * h:32 * h + 32, :], v_aug[:, j, u * UH + 4 * q + h, :],
                                            probs[:, (g % 2) * 4 + h, :], start=(g % GROUPS == 0),
                                            stop=(g % GROUPS == GROUPS - 1))
                last.then_inc(s_pv, 1)

            def turned(src, n=TT):
                to = free()
                for k in range(n):
                    last = nc.tensor.transpose(to[:, k * P:(k + 1) * P], src(k), ident[:])
                done(last)

            def output_sums(b, u):
                pe.wait_ge(s_pvo, b * UNITS + u + 1)
                turned(lambda k: pv_s[:, k * P:(k + 1) * P])

            def project(since=TT):
                pe.wait_ge(s_dd, d.value(-since))
                for half in range(2):
                    to = free()
                    for n in range(TT // 2):
                        k = half * (TT // 2) + n
                        last = nc.tensor.matmul(to[:, n * P:(n + 1) * P], attnT[:, k * P:(k + 1) * P], wo_s[:], start=True,
                                                stop=True)
                    done(last)

            def attn_turned():
                pe.wait_ge(s_dd, d.value(-TT))
                turned(lambda k: attn[:, k, :])

            def group(b, g, last=False, first=False):
                def ahead(k, n):
                    head = g + LEAD
                    if head < GB:
                        scores_for_max(b, head // UH, head % UH, k, n)
                    elif not last:
                        scores_for_max(b + 1, 0, head - GB, k, n)

                new_maxima = g % 4 == 2 and not (last and g // 4 == 3)
                ahead(0, 2)
                if g >= 2:
                    with_v(b, g - 2)
                elif not first:
                    with_v(b - 1, GB - 2 + g)
                if new_maxima:
                    maxima(b * HALVES + g // 4 + 1, (g // 4 + 1) % 2, b * GB + g)
                ahead(2, 1)
                scores(b, g, 0, 2, new_maxima, last)
                ahead(3, 1)
                scores(b, g, 2, 2, new_maxima, last)
                if g == 1 and not first:
                    output_sums(b - 1, 1)
                if g == 2 and not first:
                    attn_turned()
                if g == 3 and not first:
                    project()
                if g == GROUPS + 1:
                    output_sums(b, 0)

            def experts(b):
                def rows_in(e, c):
                    pe.wait_ge(s_xe, e * 16 + 16)
                    c0, w = CH[c]
                    turned(lambda k: xe[:, c0 // P + k, :], w // P)
                    return d.value()

                def up(e, q, chunks):
                    pe.wait_ge(s_split, e * 2 + 2)
                    for hc in range(HC):
                        for c, (c0, w) in enumerate(CH):
                            k = hc * NCH + c
                            if hc == 0:
                                pe.wait_ge(s_xhi, e * NCH + c + 1)
                            if k >= 4:
                                pe.wait_ge(s_ge, e * (HC * NCH) + k - 3)
                            hi, lo = (t[:, hc * P:(hc + 1) * P] for t in wfc_parts[q])
                            to = bA[k % 4][:, 0:w]
                            nc.tensor.matmul(to, lo, xeT[0][:, c0:c0 + w], start=True, stop=False)
                            nc.tensor.matmul(to, hi, xeT[0][:, c0:c0 + w], start=False, stop=False)
                            if hc == 0:
                                pe.wait_ge(s_dd, chunks[c])
                            nc.tensor.matmul(to, hi, xeT[1][:, c0:c0 + w], start=False, stop=True).then_inc(s_up, 1)

                def down(e, q, c):
                    c0, w = CH[c]
                    pe.wait_ge(s_ge, e * (HC * NCH) + (HC - 1) * NCH + c + 1)
                    to = free()
                    for k in range(w // P):
                        for hc in range(HC):
                            last = nc.tensor.matmul(to[:, k * P:(k + 1) * P], hid[:, hc, c0 + k * P:c0 + (k + 1) * P],
                                                    wpj[q][:, hc, :], start=(hc == 0), stop=(hc == HC - 1))
                    done(last)

                e0 = b * 2 - 2 * EXPERTS_FROM
                chunks = [rows_in(e0, c) for c in range(NCH)]
                pe.wait_ge(s_exp, b * (4 * GB) + 4 * (GB + 4))
                up(e0, 0, chunks)
                chunks = []
                for kind, c in BETWEEN:
                    if kind == "rows":
                        chunks.append(rows_in(e0 + 1, c))
                    else:
                        down(e0, 0, c)
                up(e0 + 1, 1, chunks)
                for c in range(NCH):
                    down(e0 + 1, 1, c)

            pe.wait_ge(s_ve, 2 * B)
            scores_for_max(0, 0, 0, 0, 3)

            pe.wait_ge(s_prefix, 1)
            pe.wait_ge(s_xT, B)
            pe.wait_ge(s_hot, 1)
            hot_f = hot[:].rearrange("p n e -> p (n e)")
            nc.tensor.matmul(bA[1][:], prefix_r[:], hot_f, start=True, stop=True)
            nc.tensor.matmul(bPV[:], ones_r[:], hot_f, start=True, stop=True).then_inc(s_rank, 1)

            scores_for_max(0, 0, 0, 3, TT - 3)
            for s in range(1, LEAD):
                scores_for_max(0, 0, s, 0, TT)
                if s == 4:
                    maxima(0, 0)
            pe.wait_ge(s_ne, 1)
            pe.wait_ge(s_ranks, 1)
            pe.wait_ge(s_lo, 2 * B)
            for g in range(4):
                group(0, g, first=True)

            def turn(b, with_experts, last):
                for g in range(4, GB):
                    group(b, g, last)
                if last:
                    with_v(b, GB - 2)
                    with_v(b, GB - 1)
                    output_sums(b, 1)
                    pe.wait_ge(s_dd, d.value())
                    turned(lambda k: attn[:, k, :])
                    project(0)
                    return
                for g in range(4):
                    group(b + 1, g)
                if with_experts:
                    experts(b)

            each_turn(pe, [(d, D_TURN, D_EXPERTS)], turn)


def kernel(L0_attn_x, L0_attn_wq_w, L0_attn_wq_b, L0_attn_wk_w, L0_attn_wk_b, L0_attn_wv_w, L0_attn_wv_b, L0_attn_wo_w,
           L0_attn_wo_b, L0_ffn_gate_w, L0_ffn_c_fc, L0_ffn_fc_bias, L0_ffn_c_proj, L0_ffn_proj_bias):
    import numpy as np
    import concourse.bacc as bacc
    from concourse.bass_utils import run_bass_kernel_spmd

    def turned(w):
        return np.ascontiguousarray(np.asarray(w).T)

    tail = np.zeros((5, 2, T), np.float32)
    tail[0:2, 0] = 1.0
    tail[2:4, 1] = 1.0
    tail[4] = 1.0
    keys = np.concatenate([E - np.arange(E), CAP * np.arange(E)]).astype(np.float32)
    ins = {
        "x": np.asarray(L0_attn_x).reshape(N, C),
        "wq": turned(L0_attn_wq_w), "wk": turned(L0_attn_wk_w), "wv": turned(L0_attn_wv_w),
        "gate": np.asarray(L0_ffn_gate_w), "wo": turned(L0_attn_wo_w),
        "bq": np.asarray(L0_attn_wq_b).reshape(C, 1), "bk": np.asarray(L0_attn_wk_b).reshape(C, 1),
        "bv": np.asarray(L0_attn_wv_b).reshape(1, C), "bo": np.asarray(L0_attn_wo_b).reshape(1, C),
        "c_fc": np.asarray(L0_ffn_c_fc),
        "fcb": np.ascontiguousarray(np.asarray(L0_ffn_fc_bias).reshape(E, HC, P).transpose(0, 2, 1)),
        "c_proj": np.asarray(L0_ffn_c_proj), "pjb": np.asarray(L0_ffn_proj_bias),
        "ident": np.eye(P, dtype=np.float32),
        "prefix": np.triu(np.ones((P, P), np.float32), 1),
        "keys": np.tile(keys, (P, 1)),
        "tail": tail,
    }
    nc = bacc.Bacc("TRN2", target_bir_lowering=False, num_devices=1)
    arrays, args = {}, []
    for name, a in ins.items():
        a = np.ascontiguousarray(a)
        arrays[f"in_{name}"] = a
        args.append(nc.dram_tensor(f"in_{name}", a.shape, mybir.dt.from_np(a.dtype), kind="ExternalInput").ap())
    out = nc.dram_tensor("out_0", [N, C], F32, kind="ExternalOutput").ap()
    build(nc, *args, out)
    r = run_bass_kernel_spmd(nc, [arrays], core_ids=[0])
    return r.results[0]["out_0"].reshape(B, T, C)
```
